# Optimizing a Trainium2 kernel written in Bass

```python
import numpy as np
import jax
import jax.numpy as jnp

def _softmax(x, axis=-1):
    return jax.nn.softmax(x, axis=axis)

def _gelu(x):
    return jax.nn.gelu(x, approximate=True)

def _silu(x):
    return jax.nn.silu(x)

def _sigmoid(x):
    return jax.nn.sigmoid(x)

def _layernorm(x, axis=-1, eps=1e-05):
    m = jnp.mean(x, axis=axis, keepdims=True)
    v = jnp.var(x, axis=axis, keepdims=True)
    return (x - m) / jnp.sqrt(v + eps)

def _scatter_add(tgt, idx, src, axis=0):
    return tgt.at[idx].add(src)

def _segment_sum(src, seg, n):
    return jax.ops.segment_sum(src, seg, n)
kernel_name = 'mk_metaformer_d2_conv_nchw256_r4_5c0ffc'

def setup_inputs(seed: int=0):
    np.random.seed(seed)
    _w = jnp.asarray

    def _rec_inputs():
        import jax
        import jax.numpy as jnp
        _gk = jax.random.key(seed)
        x = -0.0005153 + 1.001 * jax.random.normal(jax.random.fold_in(_gk, 1), (4, 64, 56, 56), jnp.float32)
        return x
    x = _rec_inputs()

    def _L0_conv_setup():
        import jax, jax.numpy as jnp
        import numpy as np
        K = 7
        GC = 16
        EPS = 1e-05

        def _unfold(x, k):
            B, C, H, W = x.shape
            p = (k - 1) // 2
            xp = jnp.pad(x, ((0, 0), (0, 0), (p, p), (p, p)))
            patches = jnp.stack([xp[:, :, i:i + H, j:j + W] for i in range(k) for j in range(k)], axis=2)
            return patches
        key = jax.random.key(seed)
        ks = jax.random.split(key, 4)
        B, C, H, W = (4, 64, 56, 56)
        Cr = C // 4
        G = C // GC
        return {'x': jax.random.normal(ks[0], (B, C, H, W), jnp.float32), 'conv1_w': jax.random.normal(ks[1], (Cr, C), jnp.float32) * 0.05, 'bn_gamma': jnp.ones((Cr,), jnp.float32), 'bn_beta': jnp.zeros((Cr,), jnp.float32), 'bn_mean': jnp.zeros((Cr,), jnp.float32), 'bn_var': jnp.ones((Cr,), jnp.float32), 'conv2_w': jax.random.normal(ks[2], (K * K * G, Cr), jnp.float32) * 0.05, 'conv2_b': jax.random.normal(ks[3], (K * K * G,), jnp.float32) * 0.05}
    _L0_conv_all = _L0_conv_setup()
    _L0_conv_in = {k: v for k, v in _L0_conv_all.items() if k in ('conv1_w', 'bn_gamma', 'bn_beta', 'bn_mean', 'bn_var', 'conv2_w', 'conv2_b')}
    del _L0_conv_all

    def _L0_ffn_setup():
        import jax, jax.numpy as jnp
        import numpy as np
        D_MODEL = 64
        N_EXPERTS = 16
        HIDDEN = 128
        SCALE = 0.02
        key = jax.random.key(seed)
        ks = jax.random.split(key, 5)
        x = jax.random.normal(ks[0], (4, 2048, D_MODEL), dtype=jnp.float32)
        gate_w = jax.random.normal(ks[1], (D_MODEL, N_EXPERTS), dtype=jnp.float32) * SCALE
        gate_b = jnp.zeros((N_EXPERTS,), dtype=jnp.float32)
        w1 = jax.random.normal(ks[2], (N_EXPERTS, D_MODEL, HIDDEN), dtype=jnp.float32) * SCALE
        w2 = jax.random.normal(ks[3], (N_EXPERTS, D_MODEL, HIDDEN), dtype=jnp.float32) * SCALE
        w3 = jax.random.normal(ks[4], (N_EXPERTS, HIDDEN, D_MODEL), dtype=jnp.float32) * SCALE
        return {'x': x, 'gate_w': gate_w, 'gate_b': gate_b, 'w1': w1, 'w2': w2, 'w3': w3}
    _L0_ffn_all = _L0_ffn_setup()
    _L0_ffn_in = {k: v for k, v in _L0_ffn_all.items() if k in ('gate_w', 'gate_b', 'w1', 'w2', 'w3')}
    del _L0_ffn_all

    def _L1_conv_setup():
        import jax, jax.numpy as jnp
        import numpy as np
        from jax import lax
        NUM_TERMS = 6
        LOW_RANK = 8
        KH, KW = (3, 3)
        STRIDE = (1, 1)
        PAD = ((1, 1), (1, 1))
        DN = ('NCHW', 'OIHW', 'NCHW')
        key = jax.random.key(seed)
        ks = jax.random.split(key, 6)
        B, Cin, H, W, Cout = (32, 64, 56, 56, 64)
        T, R = (NUM_TERMS, LOW_RANK)
        return {'x': jax.random.normal(ks[0], (B, Cin, H, W), dtype=jnp.float32), 'S1s': jax.random.normal(ks[1], (T * R, Cin, KH, KW), dtype=jnp.float32) * 0.05, 'S2s': jax.random.normal(ks[2], (T, R * KH * KW, Cout), dtype=jnp.float32) * 0.05, 'U1s': jax.random.normal(ks[3], (T, R, Cout), dtype=jnp.float32) * 0.05, 'U2s': jax.random.normal(ks[4], (T * R * KH * KW, Cin, KH, KW), dtype=jnp.float32) * 0.05, 'bias': jax.random.normal(ks[5], (Cout,), dtype=jnp.float32) * 0.05}
    _L1_conv_all = _L1_conv_setup()
    _L1_conv_in = {k: v for k, v in _L1_conv_all.items() if k in ('S1s', 'S2s', 'U1s', 'U2s', 'bias')}
    del _L1_conv_all

    def _L1_ffn_setup():
        import jax, jax.numpy as jnp
        import numpy as np
        from jax import lax
        key = jax.random.key(seed)
        B, T, I, H = (16, 512, 64, 64)
        ks = jax.random.split(key, 13)
        s = 1.0 / np.sqrt(H)

        def w(k, shape):
            return jax.random.uniform(k, shape, jnp.float32, -s, s)
        return {'x': jax.random.normal(ks[0], (B, T, I), jnp.float32), 'U_i': w(ks[1], (I, H)), 'V_i': w(ks[2], (H, H)), 'b_i': w(ks[3], (H,)), 'U_f': w(ks[4], (I, H)), 'V_f': w(ks[5], (H, H)), 'b_f': w(ks[6], (H,)), 'U_c': w(ks[7], (I, H)), 'V_c': w(ks[8], (H, H)), 'b_c': w(ks[9], (H,)), 'U_o': w(ks[10], (I, H)), 'V_o': w(ks[11], (H, H)), 'b_o': w(ks[12], (H,))}
    _L1_ffn_all = _L1_ffn_setup()
    _L1_ffn_in = {k: v for k, v in _L1_ffn_all.items() if k in ('U_i', 'V_i', 'b_i', 'U_f', 'V_f', 'b_f', 'U_c', 'V_c', 'b_c', 'U_o', 'V_o', 'b_o')}
    del _L1_ffn_all
    return {'x': x, 'L0_conv_conv1_w': _L0_conv_in['conv1_w'], 'L0_conv_bn_gamma': _L0_conv_in['bn_gamma'], 'L0_conv_bn_beta': _L0_conv_in['bn_beta'], 'L0_conv_bn_mean': _L0_conv_in['bn_mean'], 'L0_conv_bn_var': _L0_conv_in['bn_var'], 'L0_conv_conv2_w': _L0_conv_in['conv2_w'], 'L0_conv_conv2_b': _L0_conv_in['conv2_b'], 'L0_ffn_gate_w': _L0_ffn_in['gate_w'], 'L0_ffn_gate_b': _L0_ffn_in['gate_b'], 'L0_ffn_w1': _L0_ffn_in['w1'], 'L0_ffn_w2': _L0_ffn_in['w2'], 'L0_ffn_w3': _L0_ffn_in['w3'], 'L1_conv_S1s': _L1_conv_in['S1s'], 'L1_conv_S2s': _L1_conv_in['S2s'], 'L1_conv_U1s': _L1_conv_in['U1s'], 'L1_conv_U2s': _L1_conv_in['U2s'], 'L1_conv_bias': _L1_conv_in['bias'], 'L1_ffn_U_i': _L1_ffn_in['U_i'], 'L1_ffn_V_i': _L1_ffn_in['V_i'], 'L1_ffn_b_i': _L1_ffn_in['b_i'], 'L1_ffn_U_f': _L1_ffn_in['U_f'], 'L1_ffn_V_f': _L1_ffn_in['V_f'], 'L1_ffn_b_f': _L1_ffn_in['b_f'], 'L1_ffn_U_c': _L1_ffn_in['U_c'], 'L1_ffn_V_c': _L1_ffn_in['V_c'], 'L1_ffn_b_c': _L1_ffn_in['b_c'], 'L1_ffn_U_o': _L1_ffn_in['U_o'], 'L1_ffn_V_o': _L1_ffn_in['V_o'], 'L1_ffn_b_o': _L1_ffn_in['b_o']}

def reference(x, L0_conv_conv1_w, L0_conv_bn_gamma, L0_conv_bn_beta, L0_conv_bn_mean, L0_conv_bn_var, L0_conv_conv2_w, L0_conv_conv2_b, L0_ffn_gate_w, L0_ffn_gate_b, L0_ffn_w1, L0_ffn_w2, L0_ffn_w3, L1_conv_S1s, L1_conv_S2s, L1_conv_U1s, L1_conv_U2s, L1_conv_bias, L1_ffn_U_i, L1_ffn_V_i, L1_ffn_b_i, L1_ffn_U_f, L1_ffn_V_f, L1_ffn_b_f, L1_ffn_U_c, L1_ffn_V_c, L1_ffn_b_c, L1_ffn_U_o, L1_ffn_V_o, L1_ffn_b_o):
    import jax
    import jax.numpy as jnp

    def _L0_conv_ref(x, conv1_w, bn_gamma, bn_beta, bn_mean, bn_var, conv2_w, conv2_b):
        import jax, jax.numpy as jnp
        import numpy as np
        K = 7
        GC = 16
        EPS = 1e-05

        def _unfold(x, k):
            B, C, H, W = x.shape
            p = (k - 1) // 2
            xp = jnp.pad(x, ((0, 0), (0, 0), (p, p), (p, p)))
            patches = jnp.stack([xp[:, :, i:i + H, j:j + W] for i in range(k) for j in range(k)], axis=2)
            return patches
        B, C, H, W = x.shape
        G = C // GC
        w = jnp.einsum('bchw,oc->bohw', x, conv1_w)
        inv_std = jax.lax.rsqrt(bn_var + EPS)
        w = (w - bn_mean[None, :, None, None]) * (bn_gamma * inv_std)[None, :, None, None] + bn_beta[None, :, None, None]
        w = jax.nn.relu(w)
        w = jnp.einsum('bchw,oc->bohw', w, conv2_w) + conv2_b[None, :, None, None]
        w = w.reshape(B, G, K * K, H, W)
        patches = _unfold(x, K).reshape(B, G, GC, K * K, H, W)
        out = jnp.einsum('bgkhw,bgckhw->bgchw', w, patches)
        return out.reshape(B, C, H, W)

    def _L0_ffn_ref(x, gate_w, gate_b, w1, w2, w3):
        import jax, jax.numpy as jnp
        import numpy as np
        D_MODEL = 64
        N_EXPERTS = 16
        HIDDEN = 128
        SCALE = 0.02
        n_experts = w1.shape[0]
        logits = jnp.einsum('bsd,de->bse', x, gate_w) + gate_b
        probs = jax.nn.softmax(logits, axis=-1)
        top_probs, top_idx = jax.lax.top_k(probs, 2)
        top_probs = top_probs / jnp.sum(top_probs, axis=-1, keepdims=True)
        dispatch = jnp.sum(jax.nn.one_hot(top_idx, n_experts, dtype=x.dtype) * top_probs[..., None], axis=-2)
        h1 = jnp.einsum('bsd,edh->bseh', x, w1)
        h2 = jnp.einsum('bsd,edh->bseh', x, w2)
        hidden = jax.nn.silu(h1) * h2
        expert_out = jnp.einsum('bseh,eho->bseo', hidden, w3)
        return jnp.einsum('bseo,bse->bso', expert_out, dispatch)

    def _L1_conv_ref(x, S1s, S2s, U1s, U2s, bias):
        import jax, jax.numpy as jnp
        import numpy as np
        from jax import lax
        NUM_TERMS = 6
        LOW_RANK = 8
        KH, KW = (3, 3)
        STRIDE = (1, 1)
        PAD = ((1, 1), (1, 1))
        DN = ('NCHW', 'OIHW', 'NCHW')
        T, R = (NUM_TERMS, LOW_RANK)
        z1 = lax.conv_general_dilated(x, S1s, STRIDE, PAD, dimension_numbers=DN)
        B, _, Ho, Wo = z1.shape
        z1 = z1.reshape(B, T, R, Ho, Wo)
        y1 = jnp.einsum('btrhw,tro->bohw', z1, U1s)
        z2 = lax.conv_general_dilated(x, U2s, STRIDE, PAD, dimension_numbers=DN)
        z2 = z2.reshape(B, T, R * KH * KW, Ho, Wo)
        y2 = jnp.einsum('btchw,tco->bohw', z2, S2s)
        return (y1 + y2) / (2.0 * T) + bias[None, :, None, None]

    def _L1_ffn_ref(x, U_i, V_i, b_i, U_f, V_f, b_f, U_c, V_c, b_c, U_o, V_o, b_o):
        import jax, jax.numpy as jnp
        import numpy as np
        from jax import lax
        B, T, _ = x.shape
        H = U_i.shape[1]
        xt = jnp.swapaxes(x, 0, 1)
        xi = xt @ U_i + b_i
        xf = xt @ U_f + b_f
        xg = xt @ U_c + b_c
        xo = xt @ U_o + b_o
        h0 = jnp.zeros((B, H), x.dtype)
        c0 = jnp.zeros((B, H), x.dtype)

        def step(carry, xs):
            h, c = carry
            xi_t, xf_t, xg_t, xo_t = xs
            i_t = jax.nn.sigmoid(xi_t + h @ V_i)
            f_t = jax.nn.sigmoid(xf_t + h @ V_f)
            g_t = jnp.tanh(xg_t + h @ V_c)
            o_t = jax.nn.sigmoid(xo_t + h @ V_o)
            c_new = h * c + i_t * g_t
            h_new = o_t * jnp.tanh(c_new)
            return ((h_new, c_new), h_new)
        (_, _), hs = lax.scan(step, (h0, c0), (xi, xf, xg, xo))
        return jnp.swapaxes(hs, 0, 1)

    def _gn(v, G=32, eps=1e-05):
        B_, C_, H_, W_ = v.shape
        g = v.reshape(B_, G, C_ // G, H_, W_)
        m = jnp.mean(g, axis=(2, 3, 4), keepdims=True)
        s = jnp.var(g, axis=(2, 3, 4), keepdims=True)
        return ((g - m) / jnp.sqrt(s + eps)).reshape(v.shape)

    def _ln_c(v, eps=1e-06):
        m = jnp.mean(v, axis=1, keepdims=True)
        s = jnp.var(v, axis=1, keepdims=True)
        return (v - m) / jnp.sqrt(s + eps)

    def _ln_t(v, eps=1e-05):
        m = jnp.mean(v, axis=-1, keepdims=True)
        s = jnp.var(v, axis=-1, keepdims=True)
        return (v - m) / jnp.sqrt(s + eps)

    def _to_tokens(v):
        B_, C_, H_, W_ = v.shape
        return v.reshape(B_, C_, H_ * W_).transpose(0, 2, 1)

    def _from_tokens(t, like):
        B_, C_, H_, W_ = like.shape
        return t.transpose(0, 2, 1).reshape(B_, C_, H_, W_)
    x = x + _L0_conv_ref(_ln_c(x), L0_conv_conv1_w, L0_conv_bn_gamma, L0_conv_bn_beta, L0_conv_bn_mean, L0_conv_bn_var, L0_conv_conv2_w, L0_conv_conv2_b)
    t = _to_tokens(x)
    t = t + _L0_ffn_ref(_ln_t(t), L0_ffn_gate_w, L0_ffn_gate_b, L0_ffn_w1, L0_ffn_w2, L0_ffn_w3)
    x = _from_tokens(t, x)
    x = x + _L1_conv_ref(_ln_c(x), L1_conv_S1s, L1_conv_S2s, L1_conv_U1s, L1_conv_U2s, L1_conv_bias)
    t = _to_tokens(x)
    t = t + _L1_ffn_ref(_ln_t(t), L1_ffn_U_i, L1_ffn_V_i, L1_ffn_b_i, L1_ffn_U_f, L1_ffn_V_f, L1_ffn_b_f, L1_ffn_U_c, L1_ffn_V_c, L1_ffn_b_c, L1_ffn_U_o, L1_ffn_V_o, L1_ffn_b_o)
    x = _from_tokens(t, x)
    return x

_drawn_inputs = setup_inputs


def setup_inputs(seed=0):
    import zlib

    import numpy as np

    out = dict(_drawn_inputs(seed))
    spreads = {'L0_conv_bn_gamma': (1.0, 0.2),
     'L0_conv_bn_beta': (0.0, 0.1),
     'L0_conv_bn_mean': (0.0, 0.1),
     'L0_conv_bn_var': (1.0, 0.591),
     'L0_ffn_gate_b': (0.0, 0.8)}
    factors = {'L0_ffn_gate_w': 8.0,
     'L0_ffn_w1': 8.0,
     'L0_ffn_w2': 8.0,
     'L0_ffn_w3': 8.0,
     'L1_ffn_V_i': 8.0,
     'L1_ffn_b_i': 8.0,
     'L1_ffn_V_c': 4.212,
     'L1_ffn_b_c': 3.553,
     'L1_ffn_V_o': 8.0,
     'L1_ffn_b_o': 8.0,
     'L1_conv_S1s': 3.01,
     'L1_conv_U1s': 2.976}
    for name, (base, spread) in spreads.items():
        noise = np.random.default_rng([zlib.crc32(name.encode()), seed]).standard_normal(out[name].shape)
        drawn = base * np.exp(spread * noise) if base else spread * noise
        out[name] = jnp.asarray(drawn.astype(out[name].dtype))
    for name, factor in factors.items():
        out[name] = (out[name] * factor).astype(out[name].dtype)
    return out
```

```python
import concourse.bass as bass
from concourse import mybir
from contextlib import ExitStack

F32 = mybir.dt.float32
F16 = mybir.dt.float16
I32 = mybir.dt.int32
U32 = mybir.dt.uint32
ACT = mybir.ActivationFunctionType
ALU = mybir.AluOpType
AX = mybir.AxisListType

B, C, H, W = 4, 64, 56, 56
Q = B // 2
TOK = Q * W
K7, PAD7 = 7, 3
G, GC, CR = 4, 16, 16
E, HID = 16, 128
TERMS, RANK = 6, 8
LR = TERMS * RANK
LK = RANK * 9
HALF = W // 2
LN_C_EPS, LN_T_EPS, BN_EPS = 1e-6, 1e-5, 1e-5
RSQRT_MAGIC = 1597463007
NEWTON = 3
CMHALF, C15, CONE, CZERO = range(4)

LEAD = 4
LAG = 5
XN_ROWS = PAD7 + H + LEAD
N3_TOP = 4
N3_ROWS = N3_TOP + H + 3
X_ROWS = H + LAG

TAPS = [(i, j0, n) for i in range(K7) for j0, n in ((0, 4), (4, 3))]
NT = len(TAPS)
EG = 2
NG = E // EG

TAP0 = 2
PRE = 16
EX0, EXP = 21, 3
CONV0 = 48


def build_program(nc, x, conv1_w, bn_gamma, bn_beta, bn_mean, bn_var, conv2_w, conv2_b, gate_w, gate_b,
                  w1, w2, w3, S1s, S2s, U1s, U2s, conv_bias, U_i, V_i, b_i, U_c, V_c, b_c, U_o, V_o, b_o, out):
    with ExitStack() as ctx:
        def sb(name, shape, dt=F32):
            return ctx.enter_context(nc.sbuf_tensor(name, shape, dt))

        def pb(name):
            return ctx.enter_context(nc.psum_tensor(name, [128, 512], F32))

        def sem(name):
            return ctx.enter_context(nc.semaphore(name))

        X = sb("X", [128, X_ROWS, Q, W])
        XN = sb("XN", [128, XN_ROWS, Q, W + 2 * PAD7])
        N3 = sb("N3", [128, N3_ROWS, Q, W + 2])
        SL = sb("SL", [128, 4, Q, W])
        XC = sb("XC", [128, 4, Q, W])
        SQ = sb("SQ", [128, 4, Q, W])
        VE = sb("VE", [128, 4, Q, W])
        RS_Y = sb("RS_Y", [128, 4, Q, W])
        RS_T = sb("RS_T", [128, 4, Q, W])
        RS_V = sb("RS_V", [128, 4, Q, W])
        CST = sb("CST", [128, 4])
        XN2 = sb("XN2", [128, TOK])
        XN4 = sb("XN4", [128, Q, W])
        RES3 = sb("RES3", [128, Q, W])
        RES4_NEXT = sb("RES4_NEXT", [128, Q, W])
        RES4 = sb("RES4", [128, Q, W])
        W1C = sb("W1C", [128, 3, 2, CR])
        REP = sb("REP", [33, 128])
        W2T = sb("W2T", [33, G * K7 * K7])
        BNV = sb("BNV", [CR, 4])
        BNT = sb("BNT", [CR, 4])
        BNS = sb("BNS", [CR, 2])
        BN = sb("BN", [96, 2])
        PM3 = sb("PM3", [96, 3, 2])
        PM = sb("PM", [128, 2])
        MHI = sb("MHI", [128, 1])
        MLO = sb("MLO", [128, 1])
        W2HI = sb("W2HI", [128, G * K7 * K7], F16)
        W2LO = sb("W2LO", [128, G * K7 * K7], F16)
        W2A = sb("W2A", [128, G * K7 * K7], F16)
        W2M = sb("W2M", [128, 2, G, K7 * K7], F16)
        WT = sb("WT", [128, K7 * K7, 2, G, GC], F16)
        RED = sb("RED", [128, TOK], F16)
        REDH = sb("REDH", [128, TOK], F16)
        REDF = sb("REDF", [128, TOK])
        PROD = sb("PROD", [128, NT, 4 * TOK])
        WM = sb("WM", [128, 2, 2, E, HID], F16)
        W3 = sb("W3", [128, E, C])
        GW = sb("GW", [128, 2, E])
        GB = sb("GB", [1, 2, E])
        SEL = sb("SEL", [64, E, HID], F16)
        DP = sb("DP", [64, 2 * TOK], F16)
        DH = sb("DH", [CR, 2 * TOK], F16)
        XS = sb("XS", [128, 2 * TOK], F16)
        XH = sb("XH", [128, 2 * TOK], F16)
        LG = sb("LG", [TOK, 2, E])
        MX = sb("MX", [TOK, 2, 8])
        NMX = sb("NMX", [TOK, 2])
        IX = sb("IX", [TOK, 2, 8], U32)
        IXF = sb("IXF", [TOK, 2, 8])
        EX = sb("EX", [TOK, 2, E])
        D1 = sb("D1", [TOK, 2, E])
        D2 = sb("D2", [TOK, 2, E])
        DS = sb("DS", [TOK, 2])
        DR = sb("DR", [TOK, 2])
        DD = sb("DD", [TOK, 2, E])
        IOTI = sb("IOTI", [TOK, E], I32)
        IOT = sb("IOT", [TOK, E])
        TH = sb("TH", [128, EG * 2 * TOK])
        UU = sb("UU", [128, EG * 2 * TOK])
        VV = sb("VV", [128, EG * 2 * TOK])
        HD = sb("HD", [128, EG, 2, TOK])
        S1 = sb("S1", [LR, C, 9])
        U1 = sb("U1", [LR, C])
        U2 = sb("U2", [108, 4, C, 9])
        S2 = sb("S2", [108, 4, C])
        WC = sb("WC", [128, 9, 128])
        CB = sb("CB", [128, 1])
        UW = sb("UW", [128, 2, 3, C])
        VW = sb("VW", [128, 3, C])
        BW = sb("BW", [1, 3, C])
        ONE = sb("ONE", [1, 2 * TOK])
        HIST = sb("HIST", [128, W, B])
        SCAN = [sb(f"SCAN{k}", [64, B, 6]) for k in range(2)]
        TO = sb("TO", [64, 2, B])
        OUT = sb("OUT", [128, Q, W])
        ID = sb("ID", [128, 128])
        IDUP = sb("IDUP", [128, 2, 128])
        MEAN = sb("MEAN", [128, 128])

        GATES = [pb(f"GATES{k}") for k in range(2)]
        CT = pb("CT")
        TAPB = pb("TAPB")
        H1B = pb("H1B")
        H2B = pb("H2B")
        DB = pb("DB")
        YB = pb("YB")
        STATE = CT[0:64, 0:24].rearrange("z (s b k) -> z s b k", s=2, k=3)
        TC = CT[0:64, 32:36]
        gi = [g[0:64, 0:HALF * B * 3].rearrange("z (t b k) -> z t b k", b=B, k=3) for g in GATES]
        go = [g[64:128, 0:HALF * B].rearrange("z (t b) -> z t b", b=B) for g in GATES]

        names = ("ld_x ld_w set_pool set_dve set_pe lead_slot lead_mean lead_xc lead_sq lead_var lead_ve lead_rs "
                 "mean xc sq var ve rs xn conv1 relu redlo tap prod acc dup logit xhi xslo gat ngmax ex dtok dT dp h1 h2 db "
                 "th1 u v hd w3 conv slots3 res3 slots2 slot1 slot0 res4 res4n "
                 "pre0 pre1 gates og ga oa hc cs th hh ocopy oadd ost dve_link mean_set rep_set").split()
        s = {n: sem(n) for n in names}
        (ld_x, ld_w, set_pool, set_dve, set_pe, lead_slot, lead_mean, lead_xc, lead_sq, lead_var, lead_ve, lead_rs,
         mean_done, xc_done, sq_done, var_done, ve_done, rs_step, xn_done, conv1_done, relu_done, redlo_done, tap_done,
         prod_done, acc_step, dup_done, logit_done, xhi_done, xslo_done, gat_step, ngmax_done, exp_done, dtok_done, dT_done, dp_step,
         h1_done, h2_done, db_done, tanh_done, u_done, v_done, hd_done, w3_done, conv_done, slot3_done, res3_done,
         slot2_done, slot1_done, slot0_done, res4_done, res4n_done, pre0_done, pre1_done, gates_done, og_done, gact_done, oact_done,
         hc_done, cell_done, tc_done, h_done, ocopy_done, oadd_done, ostored, setup_step, mean_set, rep_set) = (s[n] for n in names)

        N_X = 2 * Q
        ctx.enter_context(nc.allow_non_contiguous_dma(reason="small weights, transposed once"))
        block = ctx.enter_context(nc.Block())
        x_dram = x.rearrange("(q p) c h w -> p c q (h w)", p=2)
        XI = X[:, 0:H].rearrange("z h q w -> z q h w")
        out_v = out.rearrange("(q p) c h w -> p c h q w", p=2)

        def col(v):
            return v.rearrange("(a b) -> a b", b=1)

        def row(v):
            return v.rearrange("(a b) -> a b", a=1)

        w_loads = []
        for p in range(2):
            h = slice(64 * p, 64 * p + 64)
            w_loads += [(W1C[h, 0, p, :], conv1_w.rearrange("o c -> c o")),
                        (PROD[h, 0:5, :].rearrange("z a b -> z (a b)")[:, 0:E * HID].rearrange("z (e n) -> z e n", e=E),
                         w1.rearrange("e c n -> c e n")),
                        (PROD[h, 5:10, :].rearrange("z a b -> z (a b)")[:, 0:E * HID].rearrange("z (e n) -> z e n", e=E),
                         w2.rearrange("e c n -> c e n")),
                        (GW[h, p, :], gate_w), (GB[:, p, :], row(gate_b)), (CB[h, :], col(conv_bias))]
            w_loads += [(UW[h, p, k, :], u) for k, u in enumerate((U_c, U_i, U_o))]
        w_loads += [(W2T[0:CR, :], conv2_w.rearrange("k o -> o k")), (W2T[32:33, :], row(conv2_b))]
        w_loads += [(BNV[:, k:k + 1], col(v)) for k, v in enumerate((bn_gamma, bn_beta, bn_mean, bn_var))]
        w_loads += [(W3[:, :, :], w3.rearrange("e n c -> n e c")),
                    (S1[:, :, :], S1s.rearrange("m c a b -> m c (a b)")), (U1[:, :], U1s.rearrange("t r c -> (t r) c")),
                    (U2[:, :, :, :], U2s.rearrange("(k m) c a b -> m k c (a b)", m=108)),
                    (S2[:, :, :], S2s.rearrange("t r c -> (t r) c").rearrange("(k m) c -> m k c", m=108))]
        w_loads += [(VW[0:64, k, :], v) for k, v in enumerate((V_c, V_i, V_o))]
        w_loads += [(BW[:, k, :], row(v)) for k, v in enumerate((b_c, b_i, b_o))]

        counted = [s[n] for n in names
                   if n not in "ld_x ld_w set_pool set_dve set_pe dve_link mean_set rep_set".split()]

        @block.sync
        def _(sp):
            for c in counted:
                sp.sem_inc(c, 1)
            sp.wait_ge(set_pool, 6)
            for k, (dst, src) in enumerate(w_loads):
                sp.dma_start(dst, src).then_inc(ld_w, 16)
            with sp.Fori(0, H) as r:
                sp.wait_ge(oadd_done, 1 + 2 * r + 2)
                for p in range(2):
                    sp.dma_start(out_v[p, :, r, :, :], OUT[64 * p:64 * p + 64, :, :]).then_inc(ostored, 16)
            sp.wait_ge(ostored, 1 + 32 * H)

        def const(k, like):
            shape = list(like.shape)
            c = CST[:, k:k + 1]
            for _ in range(len(shape) - 2):
                c = c.unsqueeze(1)
            return c.broadcast_to(shape)

        def keep(pool, dst, src):
            return pool.tensor_tensor(dst, src, const(CONE, src), ALU.mult)

        def rsqrt(pool, y, t, nv, v, done, base):
            pool.tensor_tensor(nv, v, const(CMHALF, v), ALU.mult).then_inc(done, 1)
            pool.tensor_scalar(y.bitcast(I32), v.bitcast(I32), -0.5, float(RSQRT_MAGIC), ALU.mult, ALU.add).then_inc(done, 1)
            n = 2
            for _ in range(NEWTON):
                pool.wait_ge(done, 1 + base + n)
                pool.tensor_tensor(t, y, y, ALU.mult).then_inc(done, 1)
                pool.wait_ge(done, 1 + base + n + 1)
                pool.tensor_tensor(t, t, nv, ALU.mult).then_inc(done, 1)
                pool.wait_ge(done, 1 + base + n + 2)
                pool.tensor_tensor(t, t, const(C15, t), ALU.add).then_inc(done, 1)
                pool.wait_ge(done, 1 + base + n + 3)
                pool.tensor_tensor(y, y, t, ALU.mult).then_inc(done, 1)
                n += 4
            pool.wait_ge(done, 1 + base + n)

        RSN = 2 + 4 * NEWTON
        ACC = NT + 3

        def pool_row(pool, j, involution, lstm):
            if lstm:
                pool.wait_ge(oadd_done, 1 + 2 * (j - LAG))
                pool.wait_ge(res4n_done, 1 + j)
                keep(pool, RES4[:, :, :], RES4_NEXT[:, :, :]).then_inc(res4_done, 1)
            pool.wait_ge(ve_done, 1 + 2 * j + 2)
            rsqrt(pool, RS_Y[:, :, :, :], RS_T[:, :, :, :], RS_V[:, :, :, :], VE[:, :, :, :], rs_step, RSN * j)
            pool.wait_ge(logit_done, 1 + j)
            pool.wait_ge(pre0_done, 1 + j)
            if lstm:
                pool.wait_ge(pre1_done, 1 + j - LAG + 1)
            if involution:
                pool.tensor_tensor(XN[:, j + (LEAD + PAD7), :, PAD7:PAD7 + W], XC[:, 0], RS_Y[:, 0], ALU.mult)
            pool.tensor_tensor(XN2[:, :].rearrange("z (q w) -> z q w", q=Q), XC[:, 1], RS_Y[:, 1], ALU.mult)
            pool.tensor_tensor(N3[:, j + (N3_TOP - 2), :, 1:1 + W], XC[:, 2], RS_Y[:, 2], ALU.mult)
            pool.tensor_tensor(XN4[:, :, :], XC[:, 3], RS_Y[:, 3], ALU.mult).then_inc(xn_done, 1)
            if lstm:
                pool.wait_ge(res4_done, 1 + j - LAG + 1)
            keep(pool, RES4_NEXT[:, :, :], SL[:, 3]).then_inc(res4n_done, 1)
            if involution:
                a = ACC * j
                for g, (_, _, n) in enumerate(TAPS):
                    if g:
                        pool.wait_ge(prod_done, 1 + NT * j + g + 1)
                        pool.wait_ge(acc_step, 1 + a + g - 1)
                        pool.tensor_tensor(PROD[:, 0, 0:n * TOK], PROD[:, 0, 0:n * TOK], PROD[:, g, 0:n * TOK],
                                           ALU.add).then_inc(acc_step, 1)
                pool.wait_ge(acc_step, 1 + a + NT - 1)
                pool.tensor_tensor(PROD[:, 0, 0:2 * TOK], PROD[:, 0, 0:2 * TOK], PROD[:, 0, 2 * TOK:4 * TOK],
                                   ALU.add).then_inc(acc_step, 1)
                pool.wait_ge(acc_step, 1 + a + NT)
                pool.tensor_tensor(PROD[:, 0, 0:TOK], PROD[:, 0, 0:TOK], PROD[:, 0, TOK:2 * TOK],
                                   ALU.add).then_inc(acc_step, 1)
                pool.wait_ge(acc_step, 1 + a + NT + 1)
                pool.tensor_tensor(PROD[:, 0, 0:TOK], PROD[:, 0, 0:TOK],
                                   X[:, j, :, :].rearrange("z q w -> z (q w)"), ALU.add).then_inc(acc_step, 1)
            if lstm:
                pool.wait_ge(ocopy_done, 1 + 4 * (j - LAG) + 2)
                pool.tensor_tensor(OUT[:, :, 0:HALF], OUT[:, :, 0:HALF], RES4[:, :, 0:HALF], ALU.add).then_inc(oadd_done, 1)
            pool.wait_ge(slot2_done, 1 + j + 1)
            if involution:
                pool.wait_ge(acc_step, 1 + ACC * j + NT + 2)
                keep(pool, SL[:, 1], PROD[:, 0, 0:TOK].rearrange("z (q w) -> z q w", q=Q)).then_inc(acc_step, 1)
                pool.tensor_copy(SL[:, 0], X[:, j + LAG, :, :]).then_inc(slot1_done, 1)
            else:
                keep(pool, SL[:, 1], const(CZERO, SL[:, 1])).then_inc(slot1_done, 1)
            if lstm:
                pool.wait_ge(ocopy_done, 1 + 4 * (j - LAG) + 4)
                pool.tensor_tensor(OUT[:, :, HALF:W], OUT[:, :, HALF:W], RES4[:, :, HALF:W], ALU.add).then_inc(oadd_done, 1)

        @block.gpsimd
        def _(pool):
            pool.memset(W1C[:, :, :, :], 0.0).then_inc(set_pool, 1)
            pool.memset(W2T[:, :], 0.0).then_inc(set_pool, 1)
            pool.memset(GW[:, :, :], 0.0).then_inc(set_pool, 1)
            for k, v in ((CMHALF, -0.5), (C15, 1.5), (CONE, 1.0), (CZERO, 0.0)):
                last = pool.memset(CST[:, k:k + 1], v)
            last.then_inc(set_pool, 1)
            pool.memset(VW[:, :, :], 0.0).then_inc(set_pool, 1)
            pool.memset(UW[:, :, :, :], 0.0).then_inc(set_pool, 1)
            pool.memset(ID[:, :], 0.0).then_inc(set_pool, 1)
            pool.wait_ge(set_pool, 7)
            pool.affine_select(out=ID[:, :], in_=ID[:, :], compare_op=ALU.not_equal, fill=1.0, base=0,
                               pattern=[[-1, 128]], channel_multiplier=1).then_inc(set_pool, 1)
            pool.memset(PM3[:, :, :], 1.0).then_inc(set_pool, 1)
            pool.wait_ge(set_pool, 9)
            pool.affine_select(out=PM3[:, :, :], in_=PM3[:, :, :], compare_op=ALU.is_ge, fill=0.0, base=0,
                               pattern=[[-32, 3], [-CR, 2]], channel_multiplier=1).then_inc(set_pool, 1)
            pool.wait_ge(set_pool, 10)
            pool.affine_select(out=PM3[:, :, :], in_=PM3[:, :, :], compare_op=ALU.is_ge, fill=0.0, base=CR - 1,
                               pattern=[[32, 3], [CR, 2]], channel_multiplier=-1).then_inc(set_pool, 1)
            pool.iota(IOTI[:, :], pattern=[[1, E]], base=0, channel_multiplier=0).then_inc(set_pool, 1)
            pool.memset(N3[:, :, :, :], 0.0).then_inc(set_pool, 1)
            pool.memset(SL[:, :, :, :], 0.0).then_inc(set_pool, 1)
            pool.memset(X[:, H:X_ROWS], 0.0).then_inc(set_pool, 1)
            pool.wait_ge(ld_w, 16 * len(w_loads))
            pool.tensor_scalar(BNT[:, 0:1], BNV[:, 3:4], BN_EPS, None, ALU.add).then_inc(set_pool, 1)
            pool.memset(BNT[:, 1:2], -0.5).then_inc(set_pool, 1)
            pool.wait_ge(set_pool, 17)
            pool.tensor_tensor(BNT[:, 2:3], BNT[:, 0:1], BNT[:, 1:2], ALU.pow).then_inc(set_pool, 1)
            pool.wait_ge(ld_x, 16 * N_X)
            pool.tensor_copy(SL[:, 0], X[:, 0, :, :]).then_inc(lead_slot, 1)
            with pool.Fori(0, LEAD) as i:
                pool.wait_ge(lead_ve, 1 + i + 1)
                rsqrt(pool, RS_Y[:, 0], RS_T[:, 0], RS_V[:, 0], VE[:, 0], lead_rs, (RSN + 1) * i)
                pool.wait_ge(set_dve, 1)
                pool.tensor_tensor(XN[:, i + PAD7, :, PAD7:PAD7 + W], XC[:, 0], RS_Y[:, 0], ALU.mult).then_inc(lead_rs, 1)
                pool.tensor_copy(SL[:, 0], X[:, i + 1, :, :]).then_inc(lead_slot, 1)
            with pool.Fori(0, LAG) as j:
                pool_row(pool, j, True, False)
            with pool.Fori(LAG, H) as j:
                pool_row(pool, j, True, True)
            with pool.Fori(H, H + LAG) as j:
                pool_row(pool, j, False, True)

        def act_fill(act, j, t, involution):
            if t == 1:
                act.wait_ge(xc_done, 1 + j + 1)
                act.activation(SQ[:, :, :, :], XC[:, :, :, :], ACT.Square).then_inc(sq_done, 1)
            if t == 3:
                act.wait_ge(var_done, 1 + j + 1)
                vb = H2B[:, 0:4 * TOK].rearrange("z (s q w) -> z s q w", s=4, q=Q)
                for k, eps in ((0, LN_C_EPS), (1, LN_T_EPS)):
                    act.activation(VE[:, k:4:2], vb[:, k:4:2], ACT.Copy, bias=eps).then_inc(ve_done, 1)
            if t == 0 and involution:
                act.wait_ge(conv1_done, 1 + j + 1)
                act.wait_ge(redlo_done, 1 + j)
                act.wait_ge(tap_done, 1 + NT * j)
                for dst, a, b in ((RED, 0, 64), (REDH, 64, 96), (REDF, 64, 96)):
                    act.activation(dst[a:b, :], TAPB[a:b, 0:TOK], ACT.Relu, scale=BN[a:b, 0:1], bias=BN[a:b, 1:2])\
                        .then_inc(relu_done, 1)
            if t == PRE:
                act.wait_ge(dup_done, 1 + j + 1)
                act.activation(XS[0:64, :], H1B[0:64, 0:2 * TOK], ACT.Copy).then_inc(xhi_done, 1)
                act.activation(XH[64:128, :], H1B[64:128, 0:2 * TOK], ACT.Copy).then_inc(xhi_done, 1)
            if t == PRE + 1:
                act.wait_ge(ngmax_done, 1 + j + 1)
                for p in range(2):
                    act.activation(EX[:, p, :], LG[:, p, :], ACT.Exp, bias=NMX[:, p:p + 1]).then_inc(exp_done, 1)
            k, r = divmod(t - EX0, EXP)
            if r == 0 and 0 <= k < NG:
                act.wait_ge(h1_done, 1 + NG * j + k + 1)
                act.activation(TH[:, :], H1B[:, 0:EG * 2 * TOK], ACT.Tanh, scale=0.5).then_inc(tanh_done, 1)

        def act_row(act, j, involution, lstm):
            for t in range(W):
                if lstm:
                    n = (j - LAG) * W + t
                    c, w = divmod(t, HALF)
                    act.wait_ge(gates_done, 1 + n + 1)
                    act.activation(SCAN[t % 2][:, :, 1:4], gi[c][:, w, :, :], ACT.Tanh).then_inc(gact_done, 1)
                    act.wait_ge(og_done, 1 + n + 1)
                    act.activation(TO[:, t % 2, :], go[c][:, w, :], ACT.Tanh).then_inc(oact_done, 1)
                    act.wait_ge(cell_done, 1 + n + 1)
                    act.activation(TC, STATE[:, t % 2, :, 2], ACT.Tanh, scale=0.5).then_inc(tc_done, 1)
                    if t == HALF + 1:
                        out_half(act, j, 0)
                act_fill(act, j, t, involution)
            if lstm:
                out_half(act, j, 1)

        def out_half(act, j, half):
            r = j - LAG
            act.wait_ge(ostored, 1 + 32 * r)
            act.wait_ge(h_done, 1 + r * W + (half + 1) * HALF)
            ws = slice(half * HALF, (half + 1) * HALF)
            for p in range(2):
                act.activation(OUT[64 * p:64 * p + 64, :, ws],
                               HIST[0:64, ws, :].rearrange("z w (q p) -> z p q w", p=2)[:, p], ACT.Copy, scale=0.5)\
                    .then_inc(ocopy_done, 1)

        @block.scalar
        def _(act):
            for p in range(2):
                for q in range(Q):
                    act.dma_start(XI[64 * p:64 * p + 64, q], x_dram[p, :, q, :].rearrange("c (h w) -> c h w", h=H))\
                        .then_inc(ld_x, 16)
            with act.Fori(0, LEAD) as i:
                act.wait_ge(lead_xc, 1 + i + 1)
                act.activation(SQ[:, 0], XC[:, 0], ACT.Square).then_inc(lead_sq, 1)
                act.wait_ge(lead_var, 1 + i + 1)
                act.activation(VE[:, 0], H2B[:, 0:TOK].rearrange("z (q w) -> z q w", q=Q), ACT.Copy, bias=LN_C_EPS)\
                    .then_inc(lead_ve, 1)
            act.wait_ge(set_dve, 3)
            with act.Fori(0, LAG) as j:
                act_row(act, j, True, False)
            with act.Fori(LAG, H) as j:
                act_row(act, j, True, True)
            with act.Fori(H, H + LAG) as j:
                act_row(act, j, False, True)

        def window(row_j, i, j0, n):
            a = XN[:, row_j + i, :, j0:j0 + W]
            return bass.AP(a.tensor, a.offset, [a.ap[0], [1, n], a.ap[1], a.ap[2]])

        GAT = 8

        def gating(dve, j, k):
            if k:
                dve.wait_ge(gat_step, 1 + GAT * j + k)
            logits = DB[0:TOK, 0:2 * E].rearrange("z (p e) -> z p e", p=2)
            if k == 0:
                dve.wait_ge(logit_done, 1 + j + 1)
                dve.tensor_copy(LG[:, :, :], logits)
                for p in range(2):
                    last = dve.max(MX[:, p, :], logits[:, p, :])
            elif k == 1:
                dve.tensor_scalar(NMX[:, :], MX[:, :, 0], -1.0, None, ALU.mult).then_inc(ngmax_done, 1)
                for p in range(2):
                    last = dve.max_index(IX[:, p, :], MX[:, p, :], LG[:, p, :])
            elif k == 2:
                last = dve.tensor_copy(IXF[:, :, :], IX[:, :, :])
            elif k == 3:
                dve.wait_ge(exp_done, 1 + 2 * j + 2)
                for p in range(2):
                    for d, m in ((D1, 0), (D2, 1)):
                        last = dve.scalar_tensor_tensor(out=d[:, p, :], in0=IOT[:, :], scalar=IXF[:, p, m:m + 1],
                                                        in1=EX[:, p, :], op0=ALU.is_equal, op1=ALU.mult)
            elif k == 4:
                last = dve.tensor_tensor(D1[:, :, :], D1[:, :, :], D2[:, :, :], ALU.add)
            elif k == 5:
                last = dve.tensor_reduce(DS[:, :], D1[:, :, :], AX.X, ALU.add)
            elif k == 6:
                last = dve.reciprocal(DR[:, :], DS[:, :])
            elif k == 7:
                dve.wait_ge(dT_done, 1 + j)
                last = dve.tensor_tensor(DD[:, :, :], D1[:, :, :], DR[:, :].unsqueeze(2).broadcast_to([TOK, 2, E]), ALU.mult)
            last.then_inc(gat_step, 1)

        def dve_fill_a(dve, j, t, involution):
            if t == 1:
                dve.wait_ge(mean_done, 1 + j + 1)
                dve.wait_ge(sq_done, 1 + j)
                dve.wait_ge(rs_step, 1 + RSN * j)
                dve.wait_ge(xn_done, 1 + j)
                dve.tensor_tensor(XC[:, :, :, :].rearrange("z s q w -> z (s q w)"),
                                  SL[:, :, :, :].rearrange("z s q w -> z (s q w)"), H1B[:, 0:4 * TOK], ALU.subtract)\
                    .then_inc(xc_done, 1)
            g = t - TAP0 - 1
            if involution and 0 <= g < NT:
                i, j0, n = TAPS[g]
                dve.wait_ge(tap_done, 1 + NT * j + g + 1)
                if g == 0:
                    dve.wait_ge(slot1_done, 1 + j)
                dve.tensor_tensor(PROD[:, g, 0:n * TOK].rearrange("z (k q w) -> z k q w", k=n, q=Q),
                                  TAPB[:, 0:n * TOK].rearrange("z (k q w) -> z k q w", k=n, q=Q),
                                  window(j, i, j0, n), ALU.mult).then_inc(prod_done, 1)
            for k in range(GAT):
                if t == PRE + 1 + k // 3:
                    gating(dve, j, k)
            if t == PRE + 5:
                dve.wait_ge(dT_done, 1 + j + 1)
                dve.wait_ge(db_done, 1 + NG * j)
                dve.tensor_copy(DP[0:E, :], DB[0:E, 0:2 * TOK]).then_inc(dp_step, 1)
                dve.tensor_copy(DH[:, :], DB[0:E, 0:2 * TOK]).then_inc(dp_step, 1)
            k, r = divmod(t - EX0, EXP)
            if r == 1 and 0 <= k < NG:
                dve.wait_ge(tanh_done, 1 + NG * j + k + 1)
                dve.wait_ge(v_done, 1 + NG * j + k)
                dve.scalar_tensor_tensor(out=UU[:, :], in0=TH[:, :], scalar=1.0, in1=H1B[:, 0:EG * 2 * TOK],
                                         op0=ALU.add, op1=ALU.mult).then_inc(u_done, 1)
            if r == 2 and 0 <= k < NG:
                dve.wait_ge(h2_done, 1 + NG * j + k + 1)
                dve.wait_ge(u_done, 1 + NG * j + k + 1)
                dve.wait_ge(hd_done, 1 + NG * j + k)
                dve.tensor_tensor(VV[:, :], UU[:, :], H2B[:, 0:EG * 2 * TOK], ALU.mult).then_inc(v_done, 1)
            if r == 0 and 0 <= k - 1 < NG:
                dve.wait_ge(db_done, 1 + NG * j + k)
                dve.wait_ge(v_done, 1 + NG * j + k)
                dve.wait_ge(w3_done, 1 + NG * j + k - 1)
                dve.tensor_tensor(HD[:, :, :, :].rearrange("z e p n -> z (e p n)"), VV[:, :], DB[:, 0:EG * 2 * TOK],
                                  ALU.mult).then_inc(hd_done, 1)

        def dve_fill_b(dve, j, t, involution):
            if t == 1 and involution:
                dve.wait_ge(relu_done, 1 + 3 * j + 3)
                dve.tensor_tensor(RED[64:96, :], REDF[64:96, :], REDH[64:96, :], ALU.subtract).then_inc(redlo_done, 1)
            if t == PRE + 1:
                dve.wait_ge(xhi_done, 1 + 2 * j + 2)
                dve.tensor_tensor(XS[64:128, :], H1B[64:128, 0:2 * TOK], XH[64:128, :], ALU.subtract).then_inc(xslo_done, 1)
            if t == PRE + 5:
                dve.wait_ge(dp_step, 1 + 3 * j + 2)
                dve.tensor_tensor(DP[32:32 + E, :], DB[0:E, 0:2 * TOK], DH[:, :], ALU.subtract).then_inc(dp_step, 1)

        def dve_end(dve, j, t):
            if t == W - 3:
                dve.wait_ge(conv_done, 1 + j + 1)
                dve.wait_ge(res4n_done, 1 + j + 1)
                dve.scalar_tensor_tensor(out=SL[:, 3], in0=TAPB[:, 0:TOK].rearrange("z (q w) -> z q w", q=Q),
                                         scalar=CB[:, 0:1], in1=RES3[:, :, :], op0=ALU.add, op1=ALU.add)\
                    .then_inc(slot3_done, 1)
            if t == W - 2:
                dve.wait_ge(slot3_done, 1 + j + 1)
                dve.tensor_copy(RES3[:, :, :], SL[:, 2]).then_inc(res3_done, 1)
            if t == W - 1:
                dve.wait_ge(w3_done, 1 + NG * (j + 1))
                dve.wait_ge(res3_done, 1 + j + 1)
                dve.tensor_tensor(SL[:, 2], SL[:, 1], YB[:, 0:TOK].rearrange("z (q w) -> z q w", q=Q), ALU.add)\
                    .then_inc(slot2_done, 1)

        def dve_row(dve, j, involution, lstm):
            for t in range(W):
                if lstm:
                    n = (j - LAG) * W + t
                    sc = SCAN[t % 2]
                    dve.wait_ge(h_done, 1 + n)
                    dve.scalar_tensor_tensor(out=sc[:, :, 5], in0=HIST[0:64, (t - 1) % W, :], scalar=0.5,
                                             in1=STATE[:, (t + 1) % 2, :, 2], op0=ALU.mult, op1=ALU.mult).then_inc(hc_done, 1)
                dve_fill_a(dve, j, t, involution)
                dve_end(dve, j, t)
                if lstm:
                    dve.wait_ge(gact_done, 1 + n + 1)
                    dve.wait_ge(hc_done, 1 + n + 1)
                    flat = sc[:, :, :].rearrange("z b k -> z (b k)")
                    dve.tensor_tensor_scan(STATE[:, t % 2, :, :].rearrange("z b k -> z (b k)"), flat[:, 0:6 * B:2],
                                           flat[:, 1:6 * B:2], 0.0, op0=ALU.mult, op1=ALU.add).then_inc(cell_done, 1)
                dve_fill_b(dve, j, t, involution)
                if lstm:
                    if t == 0:
                        dve.wait_ge(ocopy_done, 1 + 4 * (j - LAG))
                    dve.wait_ge(tc_done, 1 + n + 1)
                    dve.wait_ge(oact_done, 1 + n + 1)
                    dve.scalar_tensor_tensor(out=HIST[0:64, t, :], in0=TO[:, t % 2, :], scalar=1.0, in1=TC,
                                             op0=ALU.add, op1=ALU.mult).then_inc(h_done, 1)

        @block.vector
        def _(dve):
            dve.memset(XN[:, :, :, :], 0.0).then_inc(set_dve, 1)
            step = [0]

            def link(ins):
                step[0] += 1
                ins.then_inc(setup_step, 1)
                dve.wait_ge(setup_step, step[0])

            link(dve.memset(MEAN[:, :], 0.0))
            link(dve.memset(MEAN[0:64, 0:64], 1.0 / C))
            dve.memset(MEAN[64:128, 64:128], 1.0 / C).then_inc(mean_set, 1)
            with dve.Fori(0, LEAD) as i:
                dve.wait_ge(lead_mean, 1 + i + 1)
                dve.wait_ge(lead_rs, 1 + (RSN + 1) * i)
                dve.tensor_tensor(XC[:, 0].rearrange("z q w -> z (q w)"), SL[:, 0].rearrange("z q w -> z (q w)"),
                                  H1B[:, 0:TOK], ALU.subtract).then_inc(lead_xc, 1)
            for tile_, v in ((REP, 0.0), (PM, 1.0), (MHI, 0.0), (MLO, 0.0), (SEL, 0.0), (DP, 0.0), (RES3, 0.0),
                             (HIST, 0.0), (ONE, 1.0), (SCAN[0], 0.0), (SCAN[1], 0.0), (WC, 0.0), (IDUP, 0.0), (TH, 0.0), (RED, 1.0)):
                link(dve.memset(tile_[:], v))
            link(dve.memset(STATE, 0.0))
            for k in range(2):
                link(dve.memset(SCAN[k][:, :, 4:5], 1.0))
            dve.wait_ge(set_pool, 18)
            dve.wait_ge(ld_w, 16 * len(w_loads))
            link(dve.tensor_copy(IOT[:, :], IOTI[:, :]))
            link(dve.tensor_copy(REP[0:CR, 0:96].rearrange("z (a o) -> z a o", a=6),
                                 ID[0:CR, 0:CR].unsqueeze(1).broadcast_to([CR, 6, CR])))
            link(dve.memset(REP[32:33, 96:98], 1.0))
            link(dve.tensor_reduce(PM[0:96, :], PM3[:, :, :].rearrange("z r p -> z p r"), AX.X, ALU.add))
            link(dve.memset(MHI[0:32, :], 1.0))
            link(dve.memset(MHI[64:97, :], 1.0))
            link(dve.memset(MLO[32:64, :], 1.0))
            link(dve.tensor_copy(MLO[96:128, :], ID[96:128, 97:98]))
            for a in (0, 32):
                link(dve.tensor_copy(SEL[a:a + E, :, :], ID[a:a + E, a:a + E].unsqueeze(2).broadcast_to([E, E, HID])))
            for p in range(2):
                h = slice(64 * p, 64 * p + 64)
                for m in range(2):
                    link(dve.tensor_copy(IDUP[h, p, 64 * m:64 * m + 64], ID[h, h]))
                for rep in (1, 2):
                    link(dve.tensor_copy(W1C[h, rep, p, :], W1C[h, 0, p, :]))
            for k in range(2):
                src = PROD[:, 5 * k:5 * k + 5, :].rearrange("z a b -> z (a b)")[:, 0:E * HID].rearrange("z (e n) -> z e n", e=E)
                link(dve.tensor_copy(WM[:, k, 0], src))
                link(dve.tensor_tensor(WM[:, k, 1], src, WM[:, k, 0], ALU.subtract))
            link(dve.tensor_scalar(W3[:, :, :], W3[:, :, :], 0.5, None, ALU.mult))
            for k, (a, b) in enumerate(((1.0, 0.5), (0.5, 0.25), (0.5, 0.25))):
                link(dve.tensor_scalar(UW[:, :, k, :], UW[:, :, k, :], a, None, ALU.mult))
                link(dve.tensor_scalar(BW[:, k, :], BW[:, k, :], a, None, ALU.mult))
                link(dve.tensor_scalar(VW[:, k, :], VW[:, k, :], b, None, ALU.mult))
            link(dve.tensor_tensor(BNS[:, 0:1], BNV[:, 0:1], BNT[:, 2:3], ALU.mult))
            link(dve.tensor_tensor(BNT[:, 3:4], BNS[:, 0:1], BNV[:, 2:3], ALU.mult))
            dve.tensor_tensor(BNS[:, 1:2], BNV[:, 1:2], BNT[:, 3:4], ALU.subtract).then_inc(rep_set, 1)
            dve.wait_ge(set_pe, 1)
            link(dve.tensor_copy(BN[:, :], DB[0:96, 256:258]))
            link(dve.tensor_copy(W2HI[:, :], DB[:, 0:G * K7 * K7]))
            link(dve.tensor_tensor(W2LO[:, :], DB[:, 0:G * K7 * K7], W2HI[:, :], ALU.subtract))
            link(dve.tensor_scalar(W2A[:, :], W2HI[:, :], MHI[:, 0:1], None, ALU.mult))
            link(dve.scalar_tensor_tensor(out=W2A[:, :], in0=W2LO[:, :], scalar=MLO[:, 0:1], in1=W2A[:, :],
                                          op0=ALU.mult, op1=ALU.add))
            for p in range(2):
                link(dve.tensor_scalar(W2M[:, p].rearrange("z g k -> z (g k)"), W2A[:, :], PM[:, p:p + 1], None, ALU.mult))
            for p in range(2):
                for g in range(G):
                    link(dve.tensor_copy(WT[:, :, p, g, :],
                                         W2M[:, p, g, :].unsqueeze(2).broadcast_to([128, K7 * K7, GC])))
            dve.wait_ge(set_pe, 2)
            for p in range(2):
                h = slice(64 * p, 64 * p + 64)
                link(dve.tensor_scalar(WC[h, 0:8, h], H1B[h, 0:8 * C].rearrange("z (k c) -> z k c", k=8),
                                       1.0 / (2 * TERMS), None, ALU.mult))
                dve.tensor_scalar(WC[h, 8, h], H2B[h, 0:C], 1.0 / (2 * TERMS), None, ALU.mult).then_inc(set_dve, 1)
            with dve.Fori(0, LAG) as j:
                dve_row(dve, j, True, False)
            with dve.Fori(LAG, H) as j:
                dve_row(dve, j, True, True)
            with dve.Fori(H, H + LAG) as j:
                dve_row(dve, j, False, True)

        def prefill(pe, c, part, done):
            g_all = gi[c].rearrange("z t b k -> z (t b) k")
            xg = gi[c].rearrange("z t (q p) k -> z p q t k", p=2)
            xo = go[c].rearrange("z t (q p) -> z p q t", p=2)
            ws = slice(c * HALF, (c + 1) * HALF)
            n = HALF * B
            if part == 0:
                pe.matmul(g_all[:, :, 0:3:2], BW[0:1, 0, :], ONE[0:1, 0:2 * n].rearrange("z (a b) -> z a b", b=2),
                          start=True, stop=False, skip_group_check=True)
                pe.matmul(g_all[:, :, 1], BW[0:1, 1, :], ONE[0:1, 0:n], start=False, stop=False, skip_group_check=True)
                last = pe.matmul(go[c].rearrange("z t b -> z (t b)"), BW[0:1, 2, :], ONE[0:1, 0:n], start=True, stop=False,
                                 skip_group_check=True)
            else:
                p = part - 1
                r = XN4[:, :, ws]
                for k in (0, 2):
                    pe.matmul(xg[:, p, :, :, k], UW[:, p, 0, :], r, start=False, stop=False, skip_group_check=True)
                pe.matmul(xg[:, p, :, :, 1], UW[:, p, 1, :], r, start=False, stop=False, skip_group_check=True)
                last = pe.matmul(xo[:, p], UW[:, p, 2, :], r, start=False, stop=False, skip_group_check=True)
            if part == 2:
                last.then_inc(done, 1)

        def pe_fill(pe, j, t, involution, lstm):
            if t == 0:
                pe.wait_ge(slot1_done, 1 + j)
                pe.wait_ge(slot2_done, 1 + j)
                pe.wait_ge(u_done, 1 + NG * j)
                pe.matmul(H1B[:, 0:4 * TOK], MEAN[:, :], SL[:, :, :, :].rearrange("z s q w -> z (s q w)"),
                          start=True, stop=True).then_inc(mean_done, 1)
                if involution:
                    pe.wait_ge(slot3_done, 1 + j)
                    pe.matmul(TAPB[0:96, 0:TOK], W1C[:, :, :, :].rearrange("z r p o -> z (r p o)"),
                              XN[:, j + PAD7, :, PAD7:PAD7 + W], start=True, stop=True).then_inc(conv1_done, 1)
            if lstm and t in (1, 2, 3):
                pe.wait_ge(gact_done, 1 + (j - LAG) * W)
                prefill(pe, 1, t - 1, pre1_done)
            if t == 2:
                pe.wait_ge(sq_done, 1 + j + 1)
                pe.wait_ge(v_done, 1 + NG * j)
                pe.matmul(H2B[:, 0:4 * TOK], MEAN[:, :], SQ[:, :, :, :].rearrange("z s q w -> z (s q w)"),
                          start=True, stop=True).then_inc(var_done, 1)
            g = t - TAP0
            if involution and 0 <= g < NT:
                if g == 0:
                    pe.wait_ge(redlo_done, 1 + j + 1)
                    pe.wait_ge(relu_done, 1 + 3 * j + 3)
                i, j0, n = TAPS[g]
                pe.wait_ge(prod_done, 1 + NT * j + g)
                for m in range(n):
                    last = pe.matmul(TAPB[:, m * TOK:(m + 1) * TOK],
                                     WT[:, i * K7 + j0 + m].rearrange("z p g c -> z (p g c)"), RED[:, :],
                                     start=(m == 0), stop=True, skip_group_check=True)
                last.then_inc(tap_done, 1)
            if t == PRE:
                pe.wait_ge(xn_done, 1 + j + 1)
                pe.wait_ge(xc_done, 1 + j + 1)
                for p in range(2):
                    last = pe.matmul(H1B[:, p * TOK:(p + 1) * TOK], IDUP[:, p, :], XN2[:, :], start=True, stop=True,
                                     skip_group_check=True)
                last.then_inc(dup_done, 1)
                pe.wait_ge(hd_done, 1 + NG * j)
                pe.matmul(DB[0:TOK, 0:2 * E], ONE[0:1, 0:TOK], GB[0:1, :, :].rearrange("z p e -> z (p e)"),
                          start=True, stop=False, skip_group_check=True)
                pe.matmul(DB[0:TOK, 0:2 * E], XN2[:, :], GW[:, :, :].rearrange("z p e -> z (p e)"), start=False, stop=True,
                          skip_group_check=True).then_inc(logit_done, 1)
            if t == PRE + 4:
                pe.wait_ge(gat_step, 1 + GAT * (j + 1))
                for p in range(2):
                    last = pe.matmul(DB[0:E, p * TOK:(p + 1) * TOK], DD[:, p, :], ID[0:TOK, 0:TOK], start=True, stop=True,
                                     skip_group_check=True)
                last.then_inc(dT_done, 1)
            k, r = divmod(t - EX0, EXP)
            if r == 0 and 0 <= k < NG:
                if k == 0:
                    pe.wait_ge(xslo_done, 1 + j + 1)
                    pe.wait_ge(xhi_done, 1 + 2 * j + 2)
                pe.wait_ge(u_done, 1 + NG * j + k)
                expert_in(pe, H1B, 0, k).then_inc(h1_done, 1)
            if r == 1 and 0 <= k < NG:
                pe.wait_ge(v_done, 1 + NG * j + k)
                pe.wait_ge(ve_done, 1 + 2 * j + 2)
                expert_in(pe, H2B, 1, k).then_inc(h2_done, 1)
            if r == 2 and 0 <= k < NG:
                pe.wait_ge(hd_done, 1 + NG * j + k)
                pe.wait_ge(dp_step, 1 + 3 * j + 3)
                for m in range(EG):
                    last = pe.matmul(DB[:, m * 2 * TOK:(m + 1) * 2 * TOK], SEL[:, EG * k + m, :], DP[:, :], start=(m == 0),
                                     stop=True, skip_group_check=True)
                last.then_inc(db_done, 1)
            if r in (1, 2) and 0 <= k - 1 < NG:
                m = r - 1
                pe.wait_ge(hd_done, 1 + NG * j + k)
                if k == 1 and m == 0:
                    pe.wait_ge(slot2_done, 1 + j)
                for p in range(2):
                    last = pe.matmul(YB[64 * p:64 * p + 64, 0:TOK], W3[:, EG * (k - 1) + m, :], HD[:, m, p, :],
                                     start=(k == 1 and m == 0), stop=(k == NG and m == EG - 1), skip_group_check=True)
                if m == EG - 1:
                    last.then_inc(w3_done, 1)
            c = 2 * (t - CONV0)
            for k in (c, c + 1):
                if 0 <= k < 9:
                    di, dj = divmod(k, 3)
                    if k == 0:
                        pe.wait_ge(xn_done, 1 + j + 1)
                        if involution:
                            pe.wait_ge(prod_done, 1 + NT * j + NT)
                        else:
                            pe.wait_ge(slot3_done, 1 + j)
                    last = pe.matmul(TAPB[:, 0:TOK], WC[:, k, :], N3[:, j + (N3_TOP - 4 + di), :, dj:dj + W],
                                     start=(k == 0), stop=(k == 8), skip_group_check=True)
                    if k == 8:
                        last.then_inc(conv_done, 1)
            if t in (W - 3, W - 2, W - 1):
                if lstm:
                    pe.wait_ge(gact_done, 1 + (j - LAG) * W + HALF)
                pe.wait_ge(xn_done, 1 + j + 1)
                prefill(pe, 0, t - (W - 3), pre0_done)

        def expert_in(pe, bank, which, k):
            for m in range(EG):
                for part in range(2):
                    last = pe.matmul(bank[:, m * 2 * TOK:(m + 1) * 2 * TOK], WM[:, which, part, EG * k + m, :], XS[:, :],
                                     start=(m == 0 and part == 0), stop=(part == 1), skip_group_check=True)
            return last

        def pe_row(pe, j, involution, lstm):
            for t in range(W):
                if lstm:
                    n = (j - LAG) * W + t
                    c, w = divmod(t, HALF)
                    h = HIST[:, (t - 1) % W, :]
                    pe.wait_ge(h_done, 1 + n)
                    pe.matmul(gi[c][:, w, :, 0:3:2], VW[:, 0, :], h.unsqueeze(2).broadcast_to([128, B, 2]),
                              start=False, stop=True, skip_group_check=True)
                    pe.matmul(gi[c][:, w, :, 1], VW[:, 1, :], h, start=False, stop=True, skip_group_check=True)\
                        .then_inc(gates_done, 1)
                    pe.matmul(go[c][:, w, :], VW[:, 2, :], h, start=False, stop=True, skip_group_check=True)\
                        .then_inc(og_done, 1)
                pe_fill(pe, j, t, involution, lstm)

        @block.tensor
        def _(pe):
            pe.wait_ge(mean_set, 1)
            with pe.Fori(0, LEAD) as i:
                pe.wait_ge(lead_slot, 1 + i + 1)
                pe.wait_ge(lead_xc, 1 + i)
                pe.matmul(H1B[:, 0:TOK], MEAN[:, :], SL[:, 0].rearrange("z q w -> z (q w)"), start=True, stop=True)\
                    .then_inc(lead_mean, 1)
                pe.wait_ge(lead_sq, 1 + i + 1)
                pe.wait_ge(lead_ve, 1 + i)
                pe.matmul(H2B[:, 0:TOK], MEAN[:, :], SQ[:, 0].rearrange("z q w -> z (q w)"), start=True, stop=True)\
                    .then_inc(lead_var, 1)
            pe.wait_ge(rep_set, 1)
            pe.matmul(DB[:, 0:G * K7 * K7], REP[:, :], W2T[:, :], start=True, stop=True, skip_group_check=True)
            pe.matmul(DB[0:96, 256:258], REP[0:CR, 0:96], BNS[:, :], start=True, stop=True, skip_group_check=True)\
                .then_inc(set_pe, 1)
            pe.wait_ge(ld_w, 16 * len(w_loads))
            pe.wait_ge(lead_ve, 1 + LEAD)
            pe.wait_ge(lead_xc, 1 + LEAD)
            for k in range(9):
                bank, a = (H1B, C * k) if k < 8 else (H2B, 0)
                for p in range(2):
                    o = bank[64 * p:64 * p + 64, a:a + C]
                    last = pe.matmul(o, S1[:, :, k], U1[:, :], start=True, stop=False, skip_group_check=True)
                    for m in range(4):
                        last = pe.matmul(o, U2[:, m, :, k], S2[:, m, :], start=False, stop=(m == 3), skip_group_check=True)
            last.then_inc(set_pe, 1)
            pe.wait_ge(set_dve, 3)
            pe.wait_ge(lead_slot, 1 + LEAD + 1)
            with pe.Fori(0, LAG) as j:
                pe_row(pe, j, True, False)
            with pe.Fori(LAG, H) as j:
                pe_row(pe, j, True, True)
            with pe.Fori(H, H + LAG) as j:
                pe_row(pe, j, False, True)


_INS = ["x", "L0_conv_conv1_w", "L0_conv_bn_gamma", "L0_conv_bn_beta", "L0_conv_bn_mean", "L0_conv_bn_var",
        "L0_conv_conv2_w", "L0_conv_conv2_b", "L0_ffn_gate_w", "L0_ffn_gate_b", "L0_ffn_w1", "L0_ffn_w2", "L0_ffn_w3",
        "L1_conv_S1s", "L1_conv_S2s", "L1_conv_U1s", "L1_conv_U2s", "L1_conv_bias",
        "L1_ffn_U_i", "L1_ffn_V_i", "L1_ffn_b_i", "L1_ffn_U_c", "L1_ffn_V_c", "L1_ffn_b_c",
        "L1_ffn_U_o", "L1_ffn_V_o", "L1_ffn_b_o"]


def kernel(**inputs):
    import numpy as _np
    import concourse.bacc as _bacc
    from concourse import mybir as _mybir
    from concourse.bass_utils import run_bass_kernel_spmd as _run

    nc = _bacc.Bacc("TRN2", target_bir_lowering=False, num_devices=1)
    arrays, args = {}, []
    for name in _INS:
        a = _np.ascontiguousarray(inputs[name])
        arrays[f"in_{name}_dram"] = a
        args.append(nc.dram_tensor(f"in_{name}_dram", a.shape, _mybir.dt.from_np(a.dtype), kind="ExternalInput").ap())
    args.append(nc.dram_tensor("out_0_dram", (B, C, H, W), F32, kind="ExternalOutput").ap())
    build_program(nc, *args)
    r = _run(nc, [arrays], core_ids=[0])
    return r.results[0]["out_0_dram"]
```

```python
import concourse.bass as bass
from concourse import mybir
from contextlib import ExitStack

F32 = mybir.dt.float32
F16 = mybir.dt.float16
I32 = mybir.dt.int32
U32 = mybir.dt.uint32
ACT = mybir.ActivationFunctionType
ALU = mybir.AluOpType
AX = mybir.AxisListType

B, C, H, W = 4, 64, 56, 56
Q = B // 2
TOK = Q * W
K7, PAD7 = 7, 3
G, GC, CR = 4, 16, 16
E, HID = 16, 128
TERMS, RANK = 6, 8
LR = TERMS * RANK
LK = RANK * 9
HALF = W // 2
LN_C_EPS, LN_T_EPS, BN_EPS = 1e-6, 1e-5, 1e-5
RSQRT_MAGIC = 1597463007
NEWTON = 3
CMHALF, C15, CONE, CZERO = range(4)

LEAD = 4
LAG = 5
XN_ROWS = PAD7 + H + LEAD
N3_TOP = 4
N3_ROWS = N3_TOP + H + 3
X_ROWS = H + LAG

TAPS = [(i, j0, n) for i in range(K7) for j0, n in ((0, 4), (4, 3))]
NT = len(TAPS)
EG = 2
NG = E // EG

TAP0 = 4
PF1 = 4
PRE = 18
CONV = {19: (0, 1), 20: (2, 3), 21: (4, 5), 22: (6, 7), 23: (8,)}
EX0, EXP = 23, 3
OUT3, OUT2 = 27, 51
PF0 = 50
PRODUCTS = 3 + 2 * 4


def build_program(nc, x, conv1_w, bn_gamma, bn_beta, bn_mean, bn_var, conv2_w, conv2_b, gate_w, gate_b,
                  w1, w2, w3, S1s, S2s, U1s, U2s, conv_bias, U_i, V_i, b_i, U_c, V_c, b_c, U_o, V_o, b_o, out):
    with ExitStack() as ctx:
        def sb(name, shape, dt=F32):
            return ctx.enter_context(nc.sbuf_tensor(name, shape, dt))

        def pb(name):
            return ctx.enter_context(nc.psum_tensor(name, [128, 512], F32))

        def sem(name):
            return ctx.enter_context(nc.semaphore(name))

        X = sb("X", [128, X_ROWS, Q, W])
        XN = sb("XN", [128, XN_ROWS, Q, W + 2 * PAD7])
        N3 = sb("N3", [128, N3_ROWS, Q, W + 2])
        SL = sb("SL", [128, 4, Q, W])
        XC = sb("XC", [128, 4, Q, W])
        SQ = sb("SQ", [128, 4, Q, W])
        VE = sb("VE", [128, 4, Q, W])
        RS_Y = sb("RS_Y", [128, 4, Q, W])
        RS_T = sb("RS_T", [128, 4, Q, W])
        RS_V = sb("RS_V", [128, 4, Q, W])
        CST = sb("CST", [128, 4])
        XN2 = sb("XN2", [128, TOK])
        XN4 = sb("XN4", [128, Q, W])
        RES3 = sb("RES3", [128, Q, W])
        RES4_NEXT = sb("RES4_NEXT", [128, Q, W])
        RES4 = sb("RES4", [128, Q, W])
        W1C = sb("W1C", [128, 3, 2, CR])
        REP = sb("REP", [33, 128])
        W2T = sb("W2T", [33, G * K7 * K7])
        BNV = sb("BNV", [CR, 4])
        BNT = sb("BNT", [CR, 4])
        BNS = sb("BNS", [CR, 2])
        BN = sb("BN", [96, 2])
        PM3 = sb("PM3", [96, 3, 2])
        PM = sb("PM", [128, 2])
        MHI = sb("MHI", [128, 1])
        MLO = sb("MLO", [128, 1])
        W2HI = sb("W2HI", [128, G * K7 * K7], F16)
        W2LO = sb("W2LO", [128, G * K7 * K7], F16)
        W2A = sb("W2A", [128, G * K7 * K7], F16)
        W2M = sb("W2M", [128, 2, G, K7 * K7], F16)
        WT = sb("WT", [128, K7 * K7, 2, G, GC], F16)
        RED = sb("RED", [128, TOK], F16)
        REDH = sb("REDH", [128, TOK], F16)
        REDF = sb("REDF", [128, TOK])
        PROD = sb("PROD", [128, NT, 4 * TOK])
        WM = sb("WM", [128, 2, 2, E, HID], F16)
        W3 = sb("W3", [128, E, C])
        GW = sb("GW", [128, 2, E])
        GB = sb("GB", [1, 2, E])
        SEL = sb("SEL", [64, E, HID], F16)
        DP = sb("DP", [64, 2 * TOK], F16)
        DH = sb("DH", [CR, 2 * TOK], F16)
        XS = sb("XS", [128, 2 * TOK], F16)
        XH = sb("XH", [128, 2 * TOK], F16)
        LG = sb("LG", [TOK, 2, E])
        MX = sb("MX", [TOK, 2, 8])
        NMX = sb("NMX", [TOK, 2])
        IX = sb("IX", [TOK, 2, 8], U32)
        IXF = sb("IXF", [TOK, 2, 8])
        EX = sb("EX", [TOK, 2, E])
        D1 = sb("D1", [TOK, 2, E])
        D2 = sb("D2", [TOK, 2, E])
        DS = sb("DS", [TOK, 2])
        DR = sb("DR", [TOK, 2])
        DD = sb("DD", [TOK, 2, E])
        IOTI = sb("IOTI", [TOK, E], I32)
        IOT = sb("IOT", [TOK, E])
        TH = sb("TH", [128, EG * 2 * TOK])
        UU = sb("UU", [128, EG * 2 * TOK])
        VV = sb("VV", [128, EG * 2 * TOK])
        HD = sb("HD", [128, EG, 2, TOK])
        S1 = sb("S1", [LR, C, 9])
        U1 = sb("U1", [LR, C])
        U2 = sb("U2", [108, 4, C, 9])
        S2 = sb("S2", [108, 4, C])
        WC = sb("WC", [128, 9, 128])
        CB = sb("CB", [128, 1])
        UW = sb("UW", [128, 2, 3, 2, C])
        VF = sb("VF", [128, 3, C])
        VH = sb("VH", [128, 3, C], F16)
        VW = sb("VW", [128, 3, 2, C], F16)
        BW = sb("BW", [1, 3, 2, C])
        ONE = sb("ONE", [1, 2 * TOK])
        HIST = sb("HIST", [128, W, B])
        HHI = sb("HHI", [128, W, B], F16)
        HLO = sb("HLO", [128, W, B], F16)
        SCAN = [sb(f"SCAN{k}", [128, B, 6]) for k in range(2)]
        TO = sb("TO", [128, 2, B])
        OUT = sb("OUT", [128, Q, W])
        ID = sb("ID", [128, 128])
        IDUP = sb("IDUP", [128, 2, 128])
        MEAN = sb("MEAN", [128, 128])

        GATES = [pb(f"GATES{k}") for k in range(2)]
        CT = pb("CT")
        TAPB = pb("TAPB")
        H1B = pb("H1B")
        H2B = pb("H2B")
        DB = pb("DB")
        YB = pb("YB")
        STATE = CT[:, 0:24].rearrange("z (s b k) -> z s b k", s=2, k=3)
        TC = CT[:, 32:36]
        gi = [g[:, 0:HALF * B * 3].rearrange("z (t b k) -> z t b k", b=B, k=3) for g in GATES]
        go = [g[:, HALF * B * 3:HALF * B * 4].rearrange("z (t b) -> z t b", b=B) for g in GATES]

        names = ("ld_x ld_w set_pool set_dve set_pe lead_slot lead_mean lead_xc lead_sq lead_var lead_ve lead_rs "
                 "mean xc sq var ve rs xn conv1 relu redlo tap prod acc dup logit xhi xslo gat ngmax ex dtok dT dp h1 h2 db "
                 "th1 u v hd w3 conv slots3 res3 slots2 slot1 slot0 res4 res4n "
                 "pre0 pre1 gates ga oa hc cs th hh hhi hlo ocopy oadd ost dve_link mean_set rep_set").split()
        s = {n: sem(n) for n in names}
        (ld_x, ld_w, set_pool, set_dve, set_pe, lead_slot, lead_mean, lead_xc, lead_sq, lead_var, lead_ve, lead_rs,
         mean_done, xc_done, sq_done, var_done, ve_done, rs_step, xn_done, conv1_done, relu_done, redlo_done, tap_done,
         prod_done, acc_step, dup_done, logit_done, xhi_done, xslo_done, gat_step, ngmax_done, exp_done, dtok_done, dT_done, dp_step,
         h1_done, h2_done, db_done, tanh_done, u_done, v_done, hd_done, w3_done, conv_done, slot3_done, res3_done,
         slot2_done, slot1_done, slot0_done, res4_done, res4n_done, pre0_done, pre1_done, gates_done, gact_done, oact_done,
         hc_done, cell_done, tc_done, h_done, hhi_done, hlo_done, ocopy_done, oadd_done, ostored, setup_step, mean_set, rep_set) = (s[n] for n in names)

        N_X = 2 * Q
        ctx.enter_context(nc.allow_non_contiguous_dma(reason="small weights, transposed once"))
        block = ctx.enter_context(nc.Block())
        x_dram = x.rearrange("(q p) c h w -> p c q (h w)", p=2)
        XI = X[:, 0:H].rearrange("z h q w -> z q h w")
        out_v = out.rearrange("(q p) c h w -> p c h q w", p=2)

        def col(v):
            return v.rearrange("(a b) -> a b", b=1)

        def row(v):
            return v.rearrange("(a b) -> a b", a=1)

        w_loads = []
        for p in range(2):
            h = slice(64 * p, 64 * p + 64)
            w_loads += [(W1C[h, 0, p, :], conv1_w.rearrange("o c -> c o")),
                        (PROD[h, 0:5, :].rearrange("z a b -> z (a b)")[:, 0:E * HID].rearrange("z (e n) -> z e n", e=E),
                         w1.rearrange("e c n -> c e n")),
                        (PROD[h, 5:10, :].rearrange("z a b -> z (a b)")[:, 0:E * HID].rearrange("z (e n) -> z e n", e=E),
                         w2.rearrange("e c n -> c e n")),
                        (GW[h, p, :], gate_w), (GB[:, p, :], row(gate_b)), (CB[h, :], col(conv_bias))]
            w_loads += [(UW[h, p, k, m, :], u) for k, u in enumerate((U_c, U_i, U_o)) for m in range(2)]
        w_loads += [(W2T[0:CR, :], conv2_w.rearrange("k o -> o k")), (W2T[32:33, :], row(conv2_b))]
        w_loads += [(BNV[:, k:k + 1], col(v)) for k, v in enumerate((bn_gamma, bn_beta, bn_mean, bn_var))]
        w_loads += [(W3[:, :, :], w3.rearrange("e n c -> n e c")),
                    (S1[:, :, :], S1s.rearrange("m c a b -> m c (a b)")), (U1[:, :], U1s.rearrange("t r c -> (t r) c")),
                    (U2[:, :, :, :], U2s.rearrange("(k m) c a b -> m k c (a b)", m=108)),
                    (S2[:, :, :], S2s.rearrange("t r c -> (t r) c").rearrange("(k m) c -> m k c", m=108))]
        w_loads += [(VF[64 * m:64 * m + 64, k, :], v) for k, v in enumerate((V_c, V_i, V_o)) for m in range(2)]
        w_loads += [(BW[:, k, m, :], row(v)) for k, v in enumerate((b_c, b_i, b_o)) for m in range(2)]

        counted = [s[n] for n in names
                   if n not in "ld_x ld_w set_pool set_dve set_pe dve_link mean_set rep_set".split()]

        @block.sync
        def _(sp):
            for c in counted:
                sp.sem_inc(c, 16 if c is ostored else 1)
            sp.wait_ge(set_pool, 5)
            for k, (dst, src) in enumerate(w_loads):
                sp.dma_start(dst, src).then_inc(ld_w, 16)
            with sp.Fori(0, H) as r:
                sp.wait_ge(oadd_done, 1 + 2 * r + 2)
                for p in range(2):
                    sp.dma_start(out_v[p, :, r, :, :], OUT[64 * p:64 * p + 64, :, :]).then_inc(ostored, 16)
            sp.wait_ge(ostored, 16 + 32 * H)

        def const(k, like):
            shape = list(like.shape)
            c = CST[:, k:k + 1]
            for _ in range(len(shape) - 2):
                c = c.unsqueeze(1)
            return c.broadcast_to(shape)

        def keep(pool, dst, src):
            return pool.tensor_tensor(dst, src, const(CONE, src), ALU.mult)

        def rsqrt(pool, y, t, nv, v, done, base):
            pool.tensor_tensor(nv, v, const(CMHALF, v), ALU.mult).then_inc(done, 1)
            pool.tensor_scalar(y.bitcast(I32), v.bitcast(I32), -0.5, float(RSQRT_MAGIC), ALU.mult, ALU.add).then_inc(done, 1)
            n = 2
            for _ in range(NEWTON):
                pool.wait_ge(done, 1 + base + n)
                pool.tensor_tensor(t, y, y, ALU.mult).then_inc(done, 1)
                pool.wait_ge(done, 1 + base + n + 1)
                pool.tensor_tensor(t, t, nv, ALU.mult).then_inc(done, 1)
                pool.wait_ge(done, 1 + base + n + 2)
                pool.tensor_tensor(t, t, const(C15, t), ALU.add).then_inc(done, 1)
                pool.wait_ge(done, 1 + base + n + 3)
                pool.tensor_tensor(y, y, t, ALU.mult).then_inc(done, 1)
                n += 4
            pool.wait_ge(done, 1 + base + n)

        RSN = 2 + 4 * NEWTON
        ACC = NT + 3

        def pool_row(pool, j, involution, lstm):
            if lstm:
                pool.wait_ge(oadd_done, 1 + 2 * (j - LAG))
                pool.wait_ge(res4n_done, 1 + j)
                keep(pool, RES4[:, :, :], RES4_NEXT[:, :, :]).then_inc(res4_done, 1)
            pool.wait_ge(ve_done, 1 + 2 * j + 2)
            rsqrt(pool, RS_Y[:, :, :, :], RS_T[:, :, :, :], RS_V[:, :, :, :], VE[:, :, :, :], rs_step, RSN * j)
            pool.wait_ge(logit_done, 1 + j)
            pool.wait_ge(pre0_done, 1 + j)
            if lstm:
                pool.wait_ge(pre1_done, 1 + j - LAG + 1)
            if involution:
                pool.tensor_tensor(XN[:, j + (LEAD + PAD7), :, PAD7:PAD7 + W], XC[:, 0], RS_Y[:, 0], ALU.mult)
            pool.tensor_tensor(XN2[:, :].rearrange("z (q w) -> z q w", q=Q), XC[:, 1], RS_Y[:, 1], ALU.mult)
            pool.tensor_tensor(N3[:, j + (N3_TOP - 2), :, 1:1 + W], XC[:, 2], RS_Y[:, 2], ALU.mult)
            pool.tensor_tensor(XN4[:, :, :], XC[:, 3], RS_Y[:, 3], ALU.mult).then_inc(xn_done, 1)
            if lstm:
                pool.wait_ge(res4_done, 1 + j - LAG + 1)
            keep(pool, RES4_NEXT[:, :, :], SL[:, 3]).then_inc(res4n_done, 1)
            if involution:
                a = ACC * j
                for g, (_, _, n) in enumerate(TAPS):
                    if g:
                        pool.wait_ge(prod_done, 1 + NT * j + g + 1)
                        pool.wait_ge(acc_step, 1 + a + g - 1)
                        pool.tensor_tensor(PROD[:, 0, 0:n * TOK], PROD[:, 0, 0:n * TOK], PROD[:, g, 0:n * TOK],
                                           ALU.add).then_inc(acc_step, 1)
                pool.wait_ge(acc_step, 1 + a + NT - 1)
                pool.tensor_tensor(PROD[:, 0, 0:2 * TOK], PROD[:, 0, 0:2 * TOK], PROD[:, 0, 2 * TOK:4 * TOK],
                                   ALU.add).then_inc(acc_step, 1)
                pool.wait_ge(acc_step, 1 + a + NT)
                pool.tensor_tensor(PROD[:, 0, 0:TOK], PROD[:, 0, 0:TOK], PROD[:, 0, TOK:2 * TOK],
                                   ALU.add).then_inc(acc_step, 1)
                pool.wait_ge(acc_step, 1 + a + NT + 1)
                pool.tensor_tensor(PROD[:, 0, 0:TOK], PROD[:, 0, 0:TOK],
                                   X[:, j, :, :].rearrange("z q w -> z (q w)"), ALU.add).then_inc(acc_step, 1)
            if lstm:
                pool.wait_ge(ocopy_done, 1 + 4 * (j - LAG) + 2)
                pool.tensor_tensor(OUT[:, :, 0:HALF], OUT[:, :, 0:HALF], RES4[:, :, 0:HALF], ALU.add).then_inc(oadd_done, 1)
            pool.wait_ge(slot2_done, 1 + j + 1)
            if involution:
                pool.wait_ge(acc_step, 1 + ACC * j + NT + 2)
                keep(pool, SL[:, 1], PROD[:, 0, 0:TOK].rearrange("z (q w) -> z q w", q=Q)).then_inc(acc_step, 1)
                pool.tensor_copy(SL[:, 0], X[:, j + LAG, :, :]).then_inc(slot1_done, 1)
            else:
                keep(pool, SL[:, 1], const(CZERO, SL[:, 1])).then_inc(slot1_done, 1)
            if lstm:
                pool.wait_ge(ocopy_done, 1 + 4 * (j - LAG) + 4)
                pool.tensor_tensor(OUT[:, :, HALF:W], OUT[:, :, HALF:W], RES4[:, :, HALF:W], ALU.add).then_inc(oadd_done, 1)

        @block.gpsimd
        def _(pool):
            pool.memset(W1C[:, :, :, :], 0.0).then_inc(set_pool, 1)
            pool.memset(W2T[:, :], 0.0).then_inc(set_pool, 1)
            pool.memset(GW[:, :, :], 0.0).then_inc(set_pool, 1)
            for k, v in ((CMHALF, -0.5), (C15, 1.5), (CONE, 1.0), (CZERO, 0.0)):
                last = pool.memset(CST[:, k:k + 1], v)
            last.then_inc(set_pool, 1)
            pool.memset(UW[:, :, :, :, :], 0.0).then_inc(set_pool, 1)
            pool.memset(ID[:, :], 0.0).then_inc(set_pool, 1)
            pool.wait_ge(set_pool, 6)
            pool.affine_select(out=ID[:, :], in_=ID[:, :], compare_op=ALU.not_equal, fill=1.0, base=0,
                               pattern=[[-1, 128]], channel_multiplier=1).then_inc(set_pool, 1)
            pool.memset(PM3[:, :, :], 1.0).then_inc(set_pool, 1)
            pool.wait_ge(set_pool, 8)
            pool.affine_select(out=PM3[:, :, :], in_=PM3[:, :, :], compare_op=ALU.is_ge, fill=0.0, base=0,
                               pattern=[[-32, 3], [-CR, 2]], channel_multiplier=1).then_inc(set_pool, 1)
            pool.wait_ge(set_pool, 9)
            pool.affine_select(out=PM3[:, :, :], in_=PM3[:, :, :], compare_op=ALU.is_ge, fill=0.0, base=CR - 1,
                               pattern=[[32, 3], [CR, 2]], channel_multiplier=-1).then_inc(set_pool, 1)
            pool.iota(IOTI[:, :], pattern=[[1, E]], base=0, channel_multiplier=0).then_inc(set_pool, 1)
            pool.memset(N3[:, :, :, :], 0.0).then_inc(set_pool, 1)
            pool.memset(SL[:, :, :, :], 0.0).then_inc(set_pool, 1)
            pool.memset(X[:, H:X_ROWS], 0.0).then_inc(set_pool, 1)
            pool.wait_ge(ld_w, 16 * len(w_loads))
            pool.tensor_scalar(BNT[:, 0:1], BNV[:, 3:4], BN_EPS, None, ALU.add).then_inc(set_pool, 1)
            pool.memset(BNT[:, 1:2], -0.5).then_inc(set_pool, 1)
            pool.wait_ge(set_pool, 16)
            pool.tensor_tensor(BNT[:, 2:3], BNT[:, 0:1], BNT[:, 1:2], ALU.pow).then_inc(set_pool, 1)
            pool.wait_ge(ld_x, 16 * N_X)
            pool.tensor_copy(SL[:, 0], X[:, 0, :, :]).then_inc(lead_slot, 1)
            with pool.Fori(0, LEAD) as i:
                pool.wait_ge(lead_ve, 1 + i + 1)
                rsqrt(pool, RS_Y[:, 0], RS_T[:, 0], RS_V[:, 0], VE[:, 0], lead_rs, (RSN + 1) * i)
                pool.wait_ge(set_dve, 1)
                pool.tensor_tensor(XN[:, i + PAD7, :, PAD7:PAD7 + W], XC[:, 0], RS_Y[:, 0], ALU.mult).then_inc(lead_rs, 1)
                pool.tensor_copy(SL[:, 0], X[:, i + 1, :, :]).then_inc(lead_slot, 1)
            with pool.Fori(0, LAG) as j:
                pool_row(pool, j, True, False)
            with pool.Fori(LAG, H) as j:
                pool_row(pool, j, True, True)
            with pool.Fori(H, H + LAG) as j:
                pool_row(pool, j, False, True)

        def act_fill(act, j, t, involution):
            if t == 1:
                act.wait_ge(xc_done, 1 + j + 1)
                act.activation(SQ[:, :, :, :], XC[:, :, :, :], ACT.Square).then_inc(sq_done, 1)
            if t == 3:
                act.wait_ge(var_done, 1 + j + 1)
                vb = H2B[:, 0:4 * TOK].rearrange("z (s q w) -> z s q w", s=4, q=Q)
                for k, eps in ((0, LN_C_EPS), (1, LN_T_EPS)):
                    act.activation(VE[:, k:4:2], vb[:, k:4:2], ACT.Copy, bias=eps).then_inc(ve_done, 1)
            if t == 2 and involution:
                act.wait_ge(conv1_done, 1 + j + 1)
                act.wait_ge(redlo_done, 1 + j)
                act.wait_ge(tap_done, 1 + NT * j)
                for dst, a, b in ((RED, 0, 64), (REDH, 64, 96), (REDF, 64, 96)):
                    act.activation(dst[a:b, :], TAPB[a:b, 0:TOK], ACT.Relu, scale=BN[a:b, 0:1], bias=BN[a:b, 1:2])\
                        .then_inc(relu_done, 1)
            if t == PRE:
                act.wait_ge(dup_done, 1 + j + 1)
                act.activation(XS[0:64, :], H1B[0:64, 0:2 * TOK], ACT.Copy).then_inc(xhi_done, 1)
                act.activation(XH[64:128, :], H1B[64:128, 0:2 * TOK], ACT.Copy).then_inc(xhi_done, 1)
            if t == PRE + 2:
                act.wait_ge(ngmax_done, 1 + j + 1)
                for p in range(2):
                    act.activation(EX[:, p, :], LG[:, p, :], ACT.Exp, bias=NMX[:, p:p + 1]).then_inc(exp_done, 1)
            if t == PRE + 4:
                act.wait_ge(dT_done, 1 + j + 1)
                act.wait_ge(db_done, 1 + NG * j)
                for dst in (DP, DH):
                    act.activation(dst[0:E, :], DB[0:E, 0:2 * TOK], ACT.Copy).then_inc(dp_step, 1)
            k, r = divmod(t - EX0, EXP)
            if r == 0 and 0 <= k < NG:
                act.wait_ge(h1_done, 1 + NG * j + k + 1)
                act.activation(TH[:, :], H1B[:, 0:EG * 2 * TOK], ACT.Tanh, scale=0.5).then_inc(tanh_done, 1)

        def act_row(act, j, involution, lstm):
            for t in range(W):
                if lstm:
                    n = (j - LAG) * W + t
                    c, w = divmod(t, HALF)
                    act.wait_ge(gates_done, 1 + n + 1)
                    act.activation(SCAN[t % 2][:, :, 1:4], gi[c][:, w, :, :], ACT.Tanh).then_inc(gact_done, 1)
                    act.activation(TO[:, t % 2, :], go[c][:, w, :], ACT.Tanh).then_inc(oact_done, 1)
                    act.wait_ge(cell_done, 1 + n + 1)
                    act.activation(TC, STATE[:, t % 2, :, 2], ACT.Tanh, scale=0.5).then_inc(tc_done, 1)
                    if t == HALF + 1:
                        out_half(act, j, 0)
                act_fill(act, j, t, involution)
            if lstm:
                out_half(act, j, 1)

        def out_half(act, j, half):
            r = j - LAG
            act.wait_ge(ostored, 16 + 32 * r)
            act.wait_ge(h_done, 1 + r * W + (half + 1) * HALF)
            ws = slice(half * HALF, (half + 1) * HALF)
            for p in range(2):
                act.activation(OUT[64 * p:64 * p + 64, :, ws],
                               HIST[0:64, ws, :].rearrange("z w (q p) -> z p q w", p=2)[:, p], ACT.Copy, scale=0.5)\
                    .then_inc(ocopy_done, 1)

        @block.scalar
        def _(act):
            for p in range(2):
                for q in range(Q):
                    act.dma_start(XI[64 * p:64 * p + 64, q], x_dram[p, :, q, :].rearrange("c (h w) -> c h w", h=H))\
                        .then_inc(ld_x, 16)
            with act.Fori(0, LEAD) as i:
                act.wait_ge(lead_xc, 1 + i + 1)
                act.activation(SQ[:, 0], XC[:, 0], ACT.Square).then_inc(lead_sq, 1)
                act.wait_ge(lead_var, 1 + i + 1)
                act.activation(VE[:, 0], H2B[:, 0:TOK].rearrange("z (q w) -> z q w", q=Q), ACT.Copy, bias=LN_C_EPS)\
                    .then_inc(lead_ve, 1)
            act.wait_ge(set_dve, 3)
            with act.Fori(0, LAG) as j:
                act_row(act, j, True, False)
            with act.Fori(LAG, H) as j:
                act_row(act, j, True, True)
            with act.Fori(H, H + LAG) as j:
                act_row(act, j, False, True)

        def window(row_j, i, j0, n):
            a = XN[:, row_j + i, :, j0:j0 + W]
            return bass.AP(a.tensor, a.offset, [a.ap[0], [1, n], a.ap[1], a.ap[2]])

        GAT = 8

        def gating(dve, j, k):
            if k:
                dve.wait_ge(gat_step, 1 + GAT * j + k)
            logits = DB[0:TOK, 0:2 * E].rearrange("z (p e) -> z p e", p=2)
            if k == 0:
                dve.wait_ge(logit_done, 1 + j + 1)
                dve.tensor_copy(LG[:, :, :], logits)
                for p in range(2):
                    last = dve.max(MX[:, p, :], logits[:, p, :])
            elif k == 1:
                dve.tensor_scalar(NMX[:, :], MX[:, :, 0], -1.0, None, ALU.mult).then_inc(ngmax_done, 1)
                for p in range(2):
                    last = dve.max_index(IX[:, p, :], MX[:, p, :], LG[:, p, :])
            elif k == 2:
                last = dve.tensor_copy(IXF[:, :, :], IX[:, :, :])
            elif k == 3:
                dve.wait_ge(exp_done, 1 + 2 * j + 2)
                for p in range(2):
                    for d, m in ((D1, 0), (D2, 1)):
                        last = dve.scalar_tensor_tensor(out=d[:, p, :], in0=IOT[:, :], scalar=IXF[:, p, m:m + 1],
                                                        in1=EX[:, p, :], op0=ALU.is_equal, op1=ALU.mult)
            elif k == 4:
                last = dve.tensor_tensor(D1[:, :, :], D1[:, :, :], D2[:, :, :], ALU.add)
            elif k == 5:
                last = dve.tensor_reduce(DS[:, :], D1[:, :, :], AX.X, ALU.add)
            elif k == 6:
                last = dve.reciprocal(DR[:, :], DS[:, :])
            elif k == 7:
                dve.wait_ge(dT_done, 1 + j)
                last = dve.tensor_tensor(DD[:, :, :], D1[:, :, :], DR[:, :].unsqueeze(2).broadcast_to([TOK, 2, E]), ALU.mult)
            last.then_inc(gat_step, 1)

        def dve_fill_a(dve, j, t, involution):
            if t == 1:
                dve.wait_ge(mean_done, 1 + j + 1)
                dve.wait_ge(sq_done, 1 + j)
                dve.wait_ge(rs_step, 1 + RSN * j)
                dve.wait_ge(xn_done, 1 + j)
                dve.tensor_tensor(XC[:, :, :, :].rearrange("z s q w -> z (s q w)"),
                                  SL[:, :, :, :].rearrange("z s q w -> z (s q w)"), H1B[:, 0:4 * TOK], ALU.subtract)\
                    .then_inc(xc_done, 1)
            g = t - TAP0 - 1
            if involution and 0 <= g < NT:
                i, j0, n = TAPS[g]
                dve.wait_ge(tap_done, 1 + NT * j + g + 1)
                if g == 0:
                    dve.wait_ge(slot1_done, 1 + j)
                dve.tensor_tensor(PROD[:, g, 0:n * TOK].rearrange("z (k q w) -> z k q w", k=n, q=Q),
                                  TAPB[:, 0:n * TOK].rearrange("z (k q w) -> z k q w", k=n, q=Q),
                                  window(j, i, j0, n), ALU.mult).then_inc(prod_done, 1)
            if t == PRE + 1:
                dve.wait_ge(xhi_done, 1 + 2 * j + 2)
                dve.tensor_tensor(XS[64:128, :], H1B[64:128, 0:2 * TOK], XH[64:128, :], ALU.subtract).then_inc(xslo_done, 1)
            for k in range(GAT):
                if t == PRE + 2 + k // 3:
                    gating(dve, j, k)
            if t == PRE + 5:
                dve.wait_ge(dp_step, 1 + 3 * j + 2)
                dve.tensor_tensor(DP[32:32 + E, :], DB[0:E, 0:2 * TOK], DH[:, :], ALU.subtract).then_inc(dp_step, 1)
            k, r = divmod(t - EX0, EXP)
            if r == 2 and 0 <= k < NG:
                dve.wait_ge(tanh_done, 1 + NG * j + k + 1)
                dve.wait_ge(v_done, 1 + NG * j + k)
                dve.scalar_tensor_tensor(out=UU[:, :], in0=TH[:, :], scalar=1.0, in1=H1B[:, 0:EG * 2 * TOK],
                                         op0=ALU.add, op1=ALU.mult).then_inc(u_done, 1)
            if r == 0 and 0 <= k - 1 < NG:
                dve.wait_ge(h2_done, 1 + NG * j + k)
                dve.wait_ge(u_done, 1 + NG * j + k)
                dve.wait_ge(hd_done, 1 + NG * j + k - 1)
                dve.tensor_tensor(VV[:, :], UU[:, :], H2B[:, 0:EG * 2 * TOK], ALU.mult).then_inc(v_done, 1)
            if r == 1 and 0 <= k - 1 < NG:
                dve.wait_ge(db_done, 1 + NG * j + k)
                dve.wait_ge(v_done, 1 + NG * j + k)
                dve.wait_ge(w3_done, 1 + NG * j + k - 1)
                dve.tensor_tensor(HD[:, :, :, :].rearrange("z e p n -> z (e p n)"), VV[:, :], DB[:, 0:EG * 2 * TOK],
                                  ALU.mult).then_inc(hd_done, 1)

        def dve_fill_b(dve, j, t, involution):
            if t == 3 and involution:
                dve.wait_ge(relu_done, 1 + 3 * j + 3)
                dve.tensor_tensor(RED[64:96, :], REDF[64:96, :], REDH[64:96, :], ALU.subtract).then_inc(redlo_done, 1)

        def dve_end(dve, j, t):
            if t == OUT3:
                dve.wait_ge(conv_done, 1 + j + 1)
                dve.wait_ge(res4n_done, 1 + j + 1)
                dve.scalar_tensor_tensor(out=SL[:, 3], in0=TAPB[:, 0:TOK].rearrange("z (q w) -> z q w", q=Q),
                                         scalar=CB[:, 0:1], in1=RES3[:, :, :], op0=ALU.add, op1=ALU.add)\
                    .then_inc(slot3_done, 1)
            if t == OUT3 + 1:
                dve.wait_ge(slot3_done, 1 + j + 1)
                dve.tensor_copy(RES3[:, :, :], SL[:, 2]).then_inc(res3_done, 1)
            if t == OUT2:
                dve.wait_ge(w3_done, 1 + NG * (j + 1))
                dve.wait_ge(res3_done, 1 + j + 1)
                dve.tensor_tensor(SL[:, 2], SL[:, 1], YB[:, 0:TOK].rearrange("z (q w) -> z q w", q=Q), ALU.add)\
                    .then_inc(slot2_done, 1)

        def dve_row(dve, j, involution, lstm):
            for t in range(W):
                if lstm:
                    n = (j - LAG) * W + t
                    sc = SCAN[t % 2]
                    dve.wait_ge(h_done, 1 + n)
                    dve.scalar_tensor_tensor(out=sc[:, :, 5], in0=HIST[:, (t - 1) % W, :], scalar=0.5,
                                             in1=STATE[:, (t + 1) % 2, :, 2], op0=ALU.mult, op1=ALU.mult).then_inc(hc_done, 1)
                dve_fill_a(dve, j, t, involution)
                if lstm:
                    dve.wait_ge(gact_done, 1 + n + 1)
                    dve.wait_ge(hc_done, 1 + n + 1)
                    flat = sc[:, :, :].rearrange("z b k -> z (b k)")
                    dve.tensor_tensor_scan(STATE[:, t % 2, :, :].rearrange("z b k -> z (b k)"), flat[:, 0:6 * B:2],
                                           flat[:, 1:6 * B:2], 0.0, op0=ALU.mult, op1=ALU.add).then_inc(cell_done, 1)
                dve_fill_b(dve, j, t, involution)
                dve_end(dve, j, t)
                if lstm:
                    if t == 0:
                        dve.wait_ge(ocopy_done, 1 + 4 * (j - LAG))
                    dve.wait_ge(tc_done, 1 + n + 1)
                    dve.wait_ge(oact_done, 1 + n + 1)
                    for dst, done in ((HHI, hhi_done), (HIST, h_done)):
                        dve.scalar_tensor_tensor(out=dst[:, t, :], in0=TO[:, t % 2, :], scalar=1.0, in1=TC,
                                                 op0=ALU.add, op1=ALU.mult).then_inc(done, 1)
                    dve.wait_ge(h_done, 1 + n + 1)
                    dve.tensor_tensor(HLO[:, t, :], HIST[:, t, :], HHI[:, t, :], ALU.subtract).then_inc(hlo_done, 1)

        @block.vector
        def _(dve):
            dve.memset(XN[:, :, :, :], 0.0).then_inc(set_dve, 1)
            step = [0]

            def link(ins):
                step[0] += 1
                ins.then_inc(setup_step, 1)
                dve.wait_ge(setup_step, step[0])

            link(dve.memset(MEAN[:, :], 0.0))
            link(dve.memset(MEAN[0:64, 0:64], 1.0 / C))
            dve.memset(MEAN[64:128, 64:128], 1.0 / C).then_inc(mean_set, 1)
            with dve.Fori(0, LEAD) as i:
                dve.wait_ge(lead_mean, 1 + i + 1)
                dve.wait_ge(lead_rs, 1 + (RSN + 1) * i)
                dve.tensor_tensor(XC[:, 0].rearrange("z q w -> z (q w)"), SL[:, 0].rearrange("z q w -> z (q w)"),
                                  H1B[:, 0:TOK], ALU.subtract).then_inc(lead_xc, 1)
            for tile_, v in ((REP, 0.0), (PM, 1.0), (MHI, 0.0), (MLO, 0.0), (SEL, 0.0), (DP, 0.0), (RES3, 0.0),
                             (HIST, 0.0), (HHI, 0.0), (HLO, 0.0), (ONE, 1.0), (SCAN[0], 0.0), (SCAN[1], 0.0), (WC, 0.0), (IDUP, 0.0), (TH, 0.0), (RED, 1.0)):
                link(dve.memset(tile_[:], v))
            link(dve.memset(STATE, 0.0))
            for k in range(2):
                link(dve.memset(SCAN[k][:, :, 4:5], 1.0))
            dve.wait_ge(set_pool, 17)
            dve.wait_ge(ld_w, 16 * len(w_loads))
            link(dve.tensor_copy(IOT[:, :], IOTI[:, :]))
            link(dve.tensor_copy(REP[0:CR, 0:96].rearrange("z (a o) -> z a o", a=6),
                                 ID[0:CR, 0:CR].unsqueeze(1).broadcast_to([CR, 6, CR])))
            link(dve.memset(REP[32:33, 96:98], 1.0))
            link(dve.tensor_reduce(PM[0:96, :], PM3[:, :, :].rearrange("z r p -> z p r"), AX.X, ALU.add))
            link(dve.memset(MHI[0:32, :], 1.0))
            link(dve.memset(MHI[64:97, :], 1.0))
            link(dve.memset(MLO[32:64, :], 1.0))
            link(dve.tensor_copy(MLO[96:128, :], ID[96:128, 97:98]))
            for a in (0, 32):
                link(dve.tensor_copy(SEL[a:a + E, :, :], ID[a:a + E, a:a + E].unsqueeze(2).broadcast_to([E, E, HID])))
            for p in range(2):
                h = slice(64 * p, 64 * p + 64)
                for m in range(2):
                    link(dve.tensor_copy(IDUP[h, p, 64 * m:64 * m + 64], ID[h, h]))
                for rep in (1, 2):
                    link(dve.tensor_copy(W1C[h, rep, p, :], W1C[h, 0, p, :]))
            for k in range(2):
                src = PROD[:, 5 * k:5 * k + 5, :].rearrange("z a b -> z (a b)")[:, 0:E * HID].rearrange("z (e n) -> z e n", e=E)
                link(dve.tensor_copy(WM[:, k, 0], src))
                link(dve.tensor_tensor(WM[:, k, 1], src, WM[:, k, 0], ALU.subtract))
            link(dve.tensor_scalar(W3[:, :, :], W3[:, :, :], 0.5, None, ALU.mult))
            for k, (a, b) in enumerate(((1.0, 0.5), (0.5, 0.25), (0.5, 0.25))):
                link(dve.tensor_scalar(UW[:, :, k], UW[:, :, k], a, None, ALU.mult))
                link(dve.tensor_scalar(BW[:, k], BW[:, k], a, None, ALU.mult))
                link(dve.tensor_scalar(VF[:, k, :], VF[:, k, :], b, None, ALU.mult))
            link(dve.tensor_copy(VH[:, :, :], VF[:, :, :]))
            for m in range(2):
                link(dve.tensor_copy(VW[0:64, :, m, :], VF[0:64, :, :]))
                link(dve.tensor_tensor(VW[64:128, :, m, :], VF[64:128, :, :], VH[64:128, :, :], ALU.subtract))
            link(dve.tensor_tensor(BNS[:, 0:1], BNV[:, 0:1], BNT[:, 2:3], ALU.mult))
            link(dve.tensor_tensor(BNT[:, 3:4], BNS[:, 0:1], BNV[:, 2:3], ALU.mult))
            dve.tensor_tensor(BNS[:, 1:2], BNV[:, 1:2], BNT[:, 3:4], ALU.subtract).then_inc(rep_set, 1)
            dve.wait_ge(set_pe, 1)
            link(dve.tensor_copy(BN[:, :], DB[0:96, 256:258]))
            link(dve.tensor_copy(W2HI[:, :], DB[:, 0:G * K7 * K7]))
            link(dve.tensor_tensor(W2LO[:, :], DB[:, 0:G * K7 * K7], W2HI[:, :], ALU.subtract))
            link(dve.tensor_scalar(W2A[:, :], W2HI[:, :], MHI[:, 0:1], None, ALU.mult))
            link(dve.scalar_tensor_tensor(out=W2A[:, :], in0=W2LO[:, :], scalar=MLO[:, 0:1], in1=W2A[:, :],
                                          op0=ALU.mult, op1=ALU.add))
            for p in range(2):
                link(dve.tensor_scalar(W2M[:, p].rearrange("z g k -> z (g k)"), W2A[:, :], PM[:, p:p + 1], None, ALU.mult))
            for p in range(2):
                for g in range(G):
                    link(dve.tensor_copy(WT[:, :, p, g, :],
                                         W2M[:, p, g, :].unsqueeze(2).broadcast_to([128, K7 * K7, GC])))
            dve.wait_ge(set_pe, 2)
            for p in range(2):
                h = slice(64 * p, 64 * p + 64)
                link(dve.tensor_scalar(WC[h, 0:8, h], H1B[h, 0:8 * C].rearrange("z (k c) -> z k c", k=8),
                                       1.0 / (2 * TERMS), None, ALU.mult))
                dve.tensor_scalar(WC[h, 8, h], H2B[h, 0:C], 1.0 / (2 * TERMS), None, ALU.mult).then_inc(set_dve, 1)
            with dve.Fori(0, LAG) as j:
                dve_row(dve, j, True, False)
            with dve.Fori(LAG, H) as j:
                dve_row(dve, j, True, True)
            with dve.Fori(H, H + LAG) as j:
                dve_row(dve, j, False, True)

        def prefill(pe, c, k, done):
            bw = BW[:, :, :, :].rearrange("z k m c -> z k (m c)")
            uw = UW[:, :, :, :, :].rearrange("z p k m c -> z p k (m c)")
            r = XN4[:, :, c * HALF:(c + 1) * HALF]
            all_g = gi[c].rearrange("z t b k -> z (t b) k")
            n = HALF * B
            if k == 0:
                last = pe.matmul(all_g[:, :, 0:3:2], bw[0:1, 0], ONE[0:1, 0:2 * n].rearrange("z (a b) -> z a b", b=2),
                                 start=True, stop=False, skip_group_check=True)
            elif k == 1:
                last = pe.matmul(all_g[:, :, 1], bw[0:1, 1], ONE[0:1, 0:n], start=False, stop=False, skip_group_check=True)
            elif k == 2:
                last = pe.matmul(go[c].rearrange("z t b -> z (t b)"), bw[0:1, 2], ONE[0:1, 0:n], start=False, stop=False,
                                 skip_group_check=True)
            else:
                p, g = divmod(k - 3, 4)
                xg = gi[c].rearrange("z t (q p) k -> z p q t k", p=2)[:, p]
                o = (xg[:, :, :, 0], xg[:, :, :, 2], xg[:, :, :, 1], go[c].rearrange("z t (q p) -> z p q t", p=2)[:, p])[g]
                last = pe.matmul(o, uw[:, p, (0, 0, 1, 2)[g]], r, start=False, stop=False, skip_group_check=True)
            if k == PRODUCTS - 1:
                last.then_inc(done, 1)

        def pe_fill(pe, j, t, involution, lstm):
            if t == 0:
                pe.wait_ge(slot1_done, 1 + j)
                pe.wait_ge(slot2_done, 1 + j)
                pe.wait_ge(slot3_done, 1 + j)
                pe.wait_ge(u_done, 1 + NG * j)
                pe.matmul(H1B[:, 0:4 * TOK], MEAN[:, :], SL[:, :, :, :].rearrange("z s q w -> z (s q w)"),
                          start=True, stop=True).then_inc(mean_done, 1)
            if t == 1 and involution:
                pe.wait_ge(slot3_done, 1 + j)
                pe.matmul(TAPB[0:96, 0:TOK], W1C[:, :, :, :].rearrange("z r p o -> z (r p o)"),
                          XN[:, j + PAD7, :, PAD7:PAD7 + W], start=True, stop=True).then_inc(conv1_done, 1)
            if lstm and 0 <= t - PF1 < PRODUCTS:
                pe.wait_ge(oact_done, 1 + (j - LAG) * W)
                prefill(pe, 1, t - PF1, pre1_done)
            if t == 2:
                pe.wait_ge(sq_done, 1 + j + 1)
                pe.wait_ge(v_done, 1 + NG * j)
                pe.matmul(H2B[:, 0:4 * TOK], MEAN[:, :], SQ[:, :, :, :].rearrange("z s q w -> z (s q w)"),
                          start=True, stop=True).then_inc(var_done, 1)
            g = t - TAP0
            if involution and 0 <= g < NT:
                if g == 0:
                    pe.wait_ge(redlo_done, 1 + j + 1)
                    pe.wait_ge(relu_done, 1 + 3 * j + 3)
                i, j0, n = TAPS[g]
                pe.wait_ge(prod_done, 1 + NT * j + g)
                for m in range(n):
                    last = pe.matmul(TAPB[:, m * TOK:(m + 1) * TOK],
                                     WT[:, i * K7 + j0 + m].rearrange("z p g c -> z (p g c)"), RED[:, :],
                                     start=(m == 0), stop=True, skip_group_check=True)
                last.then_inc(tap_done, 1)
            if t == PRE:
                pe.wait_ge(xn_done, 1 + j + 1)
                pe.wait_ge(xc_done, 1 + j + 1)
                for p in range(2):
                    last = pe.matmul(H1B[:, p * TOK:(p + 1) * TOK], IDUP[:, p, :], XN2[:, :], start=True, stop=True,
                                     skip_group_check=True)
                last.then_inc(dup_done, 1)
                pe.wait_ge(hd_done, 1 + NG * j)
                pe.matmul(DB[0:TOK, 0:2 * E], ONE[0:1, 0:TOK], GB[0:1, :, :].rearrange("z p e -> z (p e)"),
                          start=True, stop=False, skip_group_check=True)
                pe.matmul(DB[0:TOK, 0:2 * E], XN2[:, :], GW[:, :, :].rearrange("z p e -> z (p e)"), start=False, stop=True,
                          skip_group_check=True).then_inc(logit_done, 1)
            if t == PRE + 4:
                pe.wait_ge(gat_step, 1 + GAT * (j + 1))
                for p in range(2):
                    last = pe.matmul(DB[0:E, p * TOK:(p + 1) * TOK], DD[:, p, :], ID[0:TOK, 0:TOK], start=True, stop=True,
                                     skip_group_check=True)
                last.then_inc(dT_done, 1)
            k, r = divmod(t - EX0, EXP)
            if r == 0 and 0 <= k < NG:
                if k == 0:
                    pe.wait_ge(xslo_done, 1 + j + 1)
                    pe.wait_ge(xhi_done, 1 + 2 * j + 2)
                pe.wait_ge(u_done, 1 + NG * j + k)
                expert_in(pe, H1B, 0, k).then_inc(h1_done, 1)
            if r == 1 and 0 <= k < NG:
                pe.wait_ge(v_done, 1 + NG * j + k)
                pe.wait_ge(ve_done, 1 + 2 * j + 2)
                expert_in(pe, H2B, 1, k).then_inc(h2_done, 1)
            if r == 2 and 0 <= k < NG:
                pe.wait_ge(hd_done, 1 + NG * j + k)
                pe.wait_ge(dp_step, 1 + 3 * j + 3)
                for m in range(EG):
                    last = pe.matmul(DB[:, m * 2 * TOK:(m + 1) * 2 * TOK], SEL[:, EG * k + m, :], DP[:, :], start=(m == 0),
                                     stop=True, skip_group_check=True)
                last.then_inc(db_done, 1)
            if r in (1, 2) and 0 <= k - 1 < NG:
                m = r - 1
                pe.wait_ge(hd_done, 1 + NG * j + k)
                if k == 1 and m == 0:
                    pe.wait_ge(slot2_done, 1 + j)
                for p in range(2):
                    last = pe.matmul(YB[64 * p:64 * p + 64, 0:TOK], W3[:, EG * (k - 1) + m, :], HD[:, m, p, :],
                                     start=(k == 1 and m == 0), stop=(k == NG and m == EG - 1), skip_group_check=True)
                if m == EG - 1:
                    last.then_inc(w3_done, 1)
            for k in CONV.get(t, ()):
                di, dj = divmod(k, 3)
                if k == 0:
                    pe.wait_ge(xn_done, 1 + j + 1)
                    if involution:
                        pe.wait_ge(prod_done, 1 + NT * j + NT)
                    else:
                        pe.wait_ge(slot3_done, 1 + j)
                last = pe.matmul(TAPB[:, 0:TOK], WC[:, k, :], N3[:, j + (N3_TOP - 4 + di), :, dj:dj + W],
                                 start=(k == 0), stop=(k == 8), skip_group_check=True)
                if k == 8:
                    last.then_inc(conv_done, 1)
            for k in (2 * (t - PF0), 2 * (t - PF0) + 1):
                if 0 <= k < PRODUCTS:
                    if lstm:
                        pe.wait_ge(oact_done, 1 + (j - LAG) * W + HALF)
                    pe.wait_ge(xn_done, 1 + j + 1)
                    prefill(pe, 0, k, pre0_done)

        def expert_in(pe, bank, which, k):
            for m in range(EG):
                for part in range(2):
                    last = pe.matmul(bank[:, m * 2 * TOK:(m + 1) * 2 * TOK], WM[:, which, part, EG * k + m, :], XS[:, :],
                                     start=(m == 0 and part == 0), stop=(part == 1), skip_group_check=True)
            return last

        def pe_row(pe, j, involution, lstm):
            for t in range(W):
                if lstm:
                    n = (j - LAG) * W + t
                    c, w = divmod(t, HALF)
                    for digits, done in ((HHI, hhi_done), (HLO, hlo_done)):
                        h = digits[:, (t - 1) % W, :]
                        pe.wait_ge(done, 1 + n)
                        pe.matmul(go[c][:, w, :], VW[:, 2].rearrange("z m c -> z (m c)"), h, start=False, stop=True,
                                  skip_group_check=True)
                        pe.matmul(gi[c][:, w, :, 0:3:2], VW[:, 0].rearrange("z m c -> z (m c)"),
                                  h.unsqueeze(2).broadcast_to([128, B, 2]), start=False, stop=True, skip_group_check=True)
                        last = pe.matmul(gi[c][:, w, :, 1], VW[:, 1].rearrange("z m c -> z (m c)"), h, start=False,
                                         stop=True, skip_group_check=True)
                    last.then_inc(gates_done, 1)
                pe_fill(pe, j, t, involution, lstm)

        @block.tensor
        def _(pe):
            pe.wait_ge(mean_set, 1)
            with pe.Fori(0, LEAD) as i:
                pe.wait_ge(lead_slot, 1 + i + 1)
                pe.wait_ge(lead_xc, 1 + i)
                pe.matmul(H1B[:, 0:TOK], MEAN[:, :], SL[:, 0].rearrange("z q w -> z (q w)"), start=True, stop=True)\
                    .then_inc(lead_mean, 1)
                pe.wait_ge(lead_sq, 1 + i + 1)
                pe.wait_ge(lead_ve, 1 + i)
                pe.matmul(H2B[:, 0:TOK], MEAN[:, :], SQ[:, 0].rearrange("z q w -> z (q w)"), start=True, stop=True)\
                    .then_inc(lead_var, 1)
            pe.wait_ge(rep_set, 1)
            pe.matmul(DB[:, 0:G * K7 * K7], REP[:, :], W2T[:, :], start=True, stop=True, skip_group_check=True)
            pe.matmul(DB[0:96, 256:258], REP[0:CR, 0:96], BNS[:, :], start=True, stop=True, skip_group_check=True)\
                .then_inc(set_pe, 1)
            pe.wait_ge(ld_w, 16 * len(w_loads))
            pe.wait_ge(lead_ve, 1 + LEAD)
            pe.wait_ge(lead_xc, 1 + LEAD)
            for k in range(9):
                bank, a = (H1B, C * k) if k < 8 else (H2B, 0)
                for p in range(2):
                    o = bank[64 * p:64 * p + 64, a:a + C]
                    last = pe.matmul(o, S1[:, :, k], U1[:, :], start=True, stop=False, skip_group_check=True)
                    for m in range(4):
                        last = pe.matmul(o, U2[:, m, :, k], S2[:, m, :], start=False, stop=(m == 3), skip_group_check=True)
            last.then_inc(set_pe, 1)
            pe.wait_ge(set_dve, 3)
            pe.wait_ge(lead_slot, 1 + LEAD + 1)
            with pe.Fori(0, LAG) as j:
                pe_row(pe, j, True, False)
            with pe.Fori(LAG, H) as j:
                pe_row(pe, j, True, True)
            with pe.Fori(H, H + LAG) as j:
                pe_row(pe, j, False, True)


_INS = ["x", "L0_conv_conv1_w", "L0_conv_bn_gamma", "L0_conv_bn_beta", "L0_conv_bn_mean", "L0_conv_bn_var",
        "L0_conv_conv2_w", "L0_conv_conv2_b", "L0_ffn_gate_w", "L0_ffn_gate_b", "L0_ffn_w1", "L0_ffn_w2", "L0_ffn_w3",
        "L1_conv_S1s", "L1_conv_S2s", "L1_conv_U1s", "L1_conv_U2s", "L1_conv_bias",
        "L1_ffn_U_i", "L1_ffn_V_i", "L1_ffn_b_i", "L1_ffn_U_c", "L1_ffn_V_c", "L1_ffn_b_c",
        "L1_ffn_U_o", "L1_ffn_V_o", "L1_ffn_b_o"]


def kernel(**inputs):
    import numpy as _np
    import concourse.bacc as _bacc
    from concourse import mybir as _mybir
    from concourse.bass_utils import run_bass_kernel_spmd as _run

    nc = _bacc.Bacc("TRN2", target_bir_lowering=False, num_devices=1)
    arrays, args = {}, []
    for name in _INS:
        a = _np.ascontiguousarray(inputs[name])
        arrays[f"in_{name}_dram"] = a
        args.append(nc.dram_tensor(f"in_{name}_dram", a.shape, _mybir.dt.from_np(a.dtype), kind="ExternalInput").ap())
    args.append(nc.dram_tensor("out_0_dram", (B, C, H, W), F32, kind="ExternalOutput").ap())
    build_program(nc, *args)
    r = _run(nc, [arrays], core_ids=[0])
    return r.results[0]["out_0_dram"]
```

```python
import concourse.bass as bass
from concourse import mybir
from contextlib import ExitStack

F32 = mybir.dt.float32
F16 = mybir.dt.float16
I32 = mybir.dt.int32
U32 = mybir.dt.uint32
ACT = mybir.ActivationFunctionType
ALU = mybir.AluOpType
AX = mybir.AxisListType

B, C, H, W = 4, 64, 56, 56
Q = B // 2
TOK = Q * W
K7, PAD7 = 7, 3
G, GC, CR = 4, 16, 16
E, HID = 16, 128
TERMS, RANK = 6, 8
LR = TERMS * RANK
LK = 108
NK = TERMS * RANK * 9 // LK
HALF = W // 2
LN_C_EPS, LN_T_EPS, BN_EPS = 1e-6, 1e-5, 1e-5
RSQRT_MAGIC = 1597463007
NEWTON = 3
GSCALE, WSCALE = 1024.0, 64.0
CMHALF, C15, CONE, CZERO, CHALF = range(5)

LEAD = 4
LAG = 5
XN_ROWS = PAD7 + H + LEAD
N3_TOP = 4
N3_ROWS = N3_TOP + H + 3
X_ROWS = H + LAG

TAPS = [(i, j0, n) for i in range(K7) for j0, n in ((0, 4), (4, 3))]
NT = len(TAPS)
EG = 2
NG = E // EG

MEAN_AT = (0, 1)
CONV1_AT = 0
VAR_AT = (3, 4)
RSB_AT = (8, 9)
TAP_AT = [2, 5, 6, 7, 10, 14] + list(range(15, 23))
LEAD_TAP_AT = list(range(2, 2 + NT))
LOGIT_AT, DUP_AT = 11, 12
GATE_AT = ("12b", "13a", "14a", "14a", "15b", "16b", "17b", "18b", "19b")
DT_AT = 20
EX0, EXP = 23, 3
LEAD_DT_AT = EX0 + 2
CONV_AT = [EX0 + 1 + EXP * k for k in range(9)]
OUT3_AT, RES3_AT, OUT2_AT = 49, 50, 51
PRODUCTS = 4 + 2 * 3
PRE1_AT = {6: (0,), 7: (1,), 13: (2, 3), 14: (4,), 15: (5,), 16: (6,), 17: (7,), 18: (8,), 19: (9,)}
PRE0_AT = {50: (0, 1), 51: (2, 3), 52: (4, 5), 53: (6, 7), 54: (8, 9)}


def build_program(nc, x, conv1_w, bn_gamma, bn_beta, bn_mean, bn_var, conv2_w, conv2_b, gate_w, gate_b,
                  w1, w2, w3, S1s, S2s, U1s, U2s, conv_bias, U_i, V_i, b_i, U_c, V_c, b_c, U_o, V_o, b_o, out):
    with ExitStack() as ctx:
        def sb(name, shape, dt=F32):
            return ctx.enter_context(nc.sbuf_tensor(name, shape, dt))

        def pb(name):
            return ctx.enter_context(nc.psum_tensor(name, [128, 512], F32))

        def sem(name):
            return ctx.enter_context(nc.semaphore(name))

        X = sb("X", [128, X_ROWS, Q, W])
        XN = sb("XN", [128, XN_ROWS, Q, W + 2 * PAD7])
        N3 = sb("N3", [128, N3_ROWS, Q, W + 2])
        SL = sb("SL", [128, 4, Q, W])
        XC = sb("XC", [128, 4, Q, W])
        SQ = sb("SQ", [128, 4, Q, W])
        VE = sb("VE", [TOK, 4, 2])
        RS_Y = sb("RS_Y", [TOK, 4, 2])
        RS_T = sb("RS_T", [TOK, 4, 2])
        RS_V = sb("RS_V", [TOK, 4, 2])
        RSE = sb("RSE", [TOK, 4, 2, C])
        RSB = sb("RSB", [128, 4, Q, W])
        CST = sb("CST", [128, 5])
        XN2 = sb("XN2", [128, TOK])
        XN4 = sb("XN4", [128, Q, W])
        RES3 = sb("RES3", [128, Q, W])
        RES4_NEXT = sb("RES4_NEXT", [128, Q, W])
        RES4 = sb("RES4", [128, Q, W])
        W1C = sb("W1C", [128, 3, 2, CR])
        REP = sb("REP", [33, 128])
        W2T = sb("W2T", [33, G * K7 * K7])
        BNV = sb("BNV", [CR, 4])
        BNT = sb("BNT", [CR, 4])
        BNS = sb("BNS", [CR, 2])
        BN = sb("BN", [96, 2])
        PM3 = sb("PM3", [96, 3, 2])
        PM = sb("PM", [128, 2])
        MHI = sb("MHI", [128, 1])
        MLO = sb("MLO", [128, 1])
        W2HI = sb("W2HI", [128, G * K7 * K7], F16)
        W2LO = sb("W2LO", [128, G * K7 * K7], F16)
        W2A = sb("W2A", [128, G * K7 * K7], F16)
        W2M = sb("W2M", [128, 2, G, K7 * K7], F16)
        WT = sb("WT", [128, K7 * K7, 2, G, GC], F16)
        RED = sb("RED", [128, TOK], F16)
        REDF = sb("REDF", [128, TOK])
        PROD = sb("PROD", [128, NT, 4 * TOK])
        WM = sb("WM", [128, 2, 2, E, HID], F16)
        W3 = sb("W3", [128, E, C])
        GW = sb("GW", [128, 2, E])
        GB = sb("GB", [1, 2, E])
        SEL = sb("SEL", [64, 2, E, HID], F16)
        DP = sb("DP", [64, TOK], F16)
        DH = sb("DH", [2 * E, TOK], F16)
        XS = sb("XS", [128, 2 * TOK], F16)
        XH = sb("XH", [128, 2 * TOK], F16)
        LG = sb("LG", [TOK, 2, E])
        MX = sb("MX", [TOK, 2, 8])
        NMX = sb("NMX", [TOK, 2])
        IX = sb("IX", [TOK, 2, 8], U32)
        IXF = sb("IXF", [TOK, 2, 8])
        EX = sb("EX", [TOK, 2, E])
        DM = sb("DM", [TOK, 2, 2, E])
        D1 = sb("D1", [TOK, 2, E])
        DS = sb("DS", [TOK, 2])
        DR = sb("DR", [TOK, 2])
        DD = sb("DD", [TOK, 2, E])
        IOTI = sb("IOTI", [TOK, E], I32)
        IOT = sb("IOT", [TOK, E])
        TH = sb("TH", [128, EG * 2 * TOK])
        UU = sb("UU", [128, EG * 2 * TOK])
        VV = sb("VV", [128, EG * 2 * TOK])
        HD = sb("HD", [128, EG, 2, TOK])
        S1 = sb("S1", [LR, C, 9])
        U1 = sb("U1", [LR, C])
        U2 = sb("U2", [LK, NK, C, 9])
        S2 = sb("S2", [LK, NK, C])
        WC = sb("WC", [128, 9, 128])
        CB = sb("CB", [128, 1])
        UW = sb("UW", [128, 2, 3, 2, C])
        VF = sb("VF", [128, 3, C])
        VH = sb("VH", [128, 3, C], F16)
        VW = sb("VW", [128, 3, 2, C], F16)
        BW = sb("BW", [1, 3, 2, C])
        ONE = sb("ONE", [1, 2 * TOK])
        HIST = sb("HIST", [128, W, B])
        HHI = sb("HHI", [128, W, B], F16)
        HLO = sb("HLO", [128, W, B], F16)
        SCAN = [sb(f"SCAN{k}", [128, B, 6]) for k in range(2)]
        TO = sb("TO", [128, 2, B])
        OUT = sb("OUT", [128, Q, W])
        ID = sb("ID", [128, 128])
        IDUP = sb("IDUP", [128, 2, 128])
        MEAN = sb("MEAN", [128, 128])
        MEAN2 = sb("MEAN2", [128, 2])

        GATES = [pb(f"GATES{k}") for k in range(2)]
        CT = pb("CT")
        TAPB = pb("TAPB")
        H1B = pb("H1B")
        H2B = pb("H2B")
        DB = pb("DB")
        YB = pb("YB")
        STATE = CT[:, 0:24].rearrange("z (s b k) -> z s b k", s=2, k=3)
        TC = CT[:, 32:36]
        gi = [g[:, 0:HALF * B * 3].rearrange("z (t b k) -> z t b k", b=B, k=3) for g in GATES]
        go = [g[:, HALF * B * 3:HALF * B * 4].rearrange("z (t b) -> z t b", b=B) for g in GATES]

        def sems(names):
            return [sem(n) for n in names.split()]

        (ld_x, ld_rest, ld_w, ld_inv, ld_exp, set_pool, set_dve, set_pe, setup_step, mean_set, rep_set,
         wm_hi, wm_lo, lead_mean, lead_xc, lead_sq, lead_var, lead_ve, lead_rs, lead_rsb, lead_rsc, lead_xn) = sems(
            "ld_x ld_rest ld_w ld_inv ld_exp set_pool set_dve set_pe setup_step mean_set rep_set wm_hi wm_lo "
            "lead_mean lead_xc lead_sq lead_var lead_ve lead_rs lead_rsb lead_rsc lead_xn")
        (mean_done, xc_done, sq_done, var_done, ve_done, rs_step, rsb_done, rsc_done, xn_done, xn4_done) = norm_sems = sems(
            "mean_done xc_done sq_done var_done ve_done rs_step rsb_done rsc_done xn_done xn4_done")
        (conv1_done, relu_done, redlo_done, tap_done, prod_done, acc_step) = inv_sems = sems(
            "conv1_done relu_done redlo_done tap_done prod_done acc_step")
        (dup_done, logit_done, xhi_done, xslo_done, gat_step, ngmax_done, exp_done, dT_done, dp_step,
         h1_done, h2_done, tanh_done, u_done, v_done, db_done, hd_done, w3_done) = expert_sems = sems(
            "dup_done logit_done xhi_done xslo_done gat_step ngmax_done exp_done dT_done dp_step h1_done h2_done "
            "tanh_done u_done v_done db_done hd_done w3_done")
        (conv_done, slot3_done, res3_done, slot2_done, slot1_done, res4_done, res4n_done) = row_sems = sems(
            "conv_done slot3_done res3_done slot2_done slot1_done res4_done res4n_done")
        (pre0_done, pre1_done, gates_done, gact_done, oact_done, hc_done, cell_done, tc_done, hhi_done,
         h_done, hlo_done, ocopy_done, oadd_done, ostored) = lstm_sems = sems(
            "pre0_done pre1_done gates_done gact_done oact_done hc_done cell_done tc_done hhi_done h_done "
            "hlo_done ocopy_done oadd_done ostored")

        N_X = 2 * Q
        ctx.enter_context(nc.allow_non_contiguous_dma(reason="small weights, transposed once"))
        block = ctx.enter_context(nc.Block())
        x_dram = x.rearrange("(q p) c h w -> p c q h w", p=2)
        out_v = out.rearrange("(q p) c h w -> p c h q w", p=2)

        def col(v):
            return v.rearrange("(a b) -> a b", b=1)

        def row(v):
            return v.rearrange("(a b) -> a b", a=1)

        def columns_twice(a):
            return a.unsqueeze(1).broadcast_to([a.shape[0], 2, a.shape[1]])

        halves = [slice(64 * p, 64 * p + 64) for p in range(2)]
        staged = [PROD[:, 5 * k:5 * k + 5, :].rearrange("z a b -> z (a b)")[:, 0:E * HID].rearrange("z (e n) -> z e n", e=E)
                  for k in range(2)]
        FIRST = LAG + 1

        def x_loads(a, b):
            return [(X[64 * p:64 * p + 64, a:b, q, :], x_dram[p, :, q, a:b, :]) for p in range(2) for q in range(Q)]

        inv_loads = [(W1C[h, 0, p, :], conv1_w.rearrange("o c -> c o")) for p, h in enumerate(halves)]
        inv_loads += [(W2T[0:CR, :], conv2_w.rearrange("k o -> o k")), (W2T[32:33, :], row(conv2_b))]
        inv_loads += [(BNV[:, k:k + 1], col(v)) for k, v in enumerate((bn_gamma, bn_beta, bn_mean, bn_var))]
        w_loads = [(S1[:, :, :], S1s.rearrange("m c a b -> m c (a b)")), (U1[:, :], U1s.rearrange("t r c -> (t r) c")),
                   (U2[:, :, :, :], U2s.rearrange("(k m) c a b -> m k c (a b)", m=LK)),
                   (S2[:, :, :], S2s.rearrange("t r c -> (t r) c").rearrange("(k m) c -> m k c", m=LK))]
        exp_loads = [(staged[k][h], w.rearrange("e c n -> c e n")) for k, w in enumerate((w1, w2)) for h in halves]
        w_loads += [(W3[:, :, :], w3.rearrange("e n c -> n e c"))]
        for p, h in enumerate(halves):
            w_loads += [(GW[h, p, :], gate_w), (GB[:, p, :], row(gate_b)), (CB[h, :], col(conv_bias))]
            w_loads += [(UW[h, p, k, :, :], columns_twice(u)) for k, u in enumerate((U_c, U_i, U_o))]
            w_loads += [(VF[h, k, :], v) for k, v in enumerate((V_c, V_i, V_o))]
        w_loads += [(BW[:, k, :, :], columns_twice(row(v))) for k, v in enumerate((b_c, b_i, b_o))]

        counted = norm_sems + inv_sems + expert_sems + row_sems + lstm_sems

        first_pass = (h1_done, h2_done, db_done, tanh_done, u_done, v_done, hd_done, w3_done)

        @block.sync
        def _(sp):
            for c in counted:
                sp.sem_inc(c, 16 if c is ostored else 1 + NG if c in first_pass else 1)
            sp.wait_ge(set_pool, 5)
            for dst, src in inv_loads:
                sp.dma_start(dst, src).then_inc(ld_inv, 16)
            for dst, src in exp_loads:
                sp.dma_start(dst, src).then_inc(ld_exp, 16)
            for dst, src in w_loads:
                sp.dma_start(dst, src).then_inc(ld_w, 16)
            for dst, src in x_loads(FIRST, H):
                sp.dma_start(dst, src).then_inc(ld_rest, 16)
            with sp.Fori(0, H) as r:
                sp.wait_ge(oadd_done, 1 + 2 * r + 2)
                for p in range(2):
                    sp.dma_start(out_v[p, :, r, :, :], OUT[64 * p:64 * p + 64, :, :]).then_inc(ostored, 16)
            sp.wait_ge(ostored, 16 + 32 * H)

        def tap_at(lstm):
            return TAP_AT if lstm else LEAD_TAP_AT

        def dt_at(lstm):
            return DT_AT if lstm else LEAD_DT_AT

        def tap_bank(g, lstm):
            return TAPB if lstm or g % 2 == 0 else GATES[1]

        def h1_bank(k, lstm):
            return H1B if lstm or k % 2 == 0 else CT

        def const(k, like):
            shape = list(like.shape)
            c = CST[0:shape[0], k:k + 1]
            for _ in range(len(shape) - 2):
                c = c.unsqueeze(1)
            return c.broadcast_to(shape)

        def keep(pool, dst, src):
            return pool.tensor_tensor(dst, src, const(CONE, src), ALU.mult)

        def rsqrt(pool, y, t, nv, v, done, base):
            pool.tensor_tensor(nv, v, const(CMHALF, v), ALU.mult).then_inc(done, 1)
            pool.tensor_scalar(y.bitcast(I32), v.bitcast(I32), -0.5, float(RSQRT_MAGIC), ALU.mult, ALU.add).then_inc(done, 1)
            n = 2
            for _ in range(NEWTON):
                pool.wait_ge(done, base + n)
                pool.tensor_tensor(t, y, y, ALU.mult).then_inc(done, 1)
                pool.wait_ge(done, base + n + 1)
                pool.tensor_tensor(t, t, nv, ALU.mult).then_inc(done, 1)
                pool.wait_ge(done, base + n + 2)
                pool.tensor_tensor(t, t, const(C15, t), ALU.add).then_inc(done, 1)
                pool.wait_ge(done, base + n + 3)
                pool.tensor_tensor(y, y, t, ALU.mult).then_inc(done, 1)
                n += 4
            pool.wait_ge(done, base + n)
            for k in range(2):
                pool.tensor_tensor(RSE[:, 2 * k:2 * k + 2], y[:, 2 * k:2 * k + 2].unsqueeze(3).broadcast_to([TOK, 2, 2, C]),
                                   const(CONE, RSE[:, 2 * k:2 * k + 2]), ALU.mult).then_inc(done, 1)

        RSN = 4 + 4 * NEWTON
        ACC = NT + 2

        def next_inputs(pool, j, lstm):
            pool.wait_ge(pre0_done, 1 + j)
            if lstm:
                pool.wait_ge(pre1_done, 1 + j - LAG + 1)
            pool.tensor_tensor(XN4[:, :, :], XC[:, 3], RSB[:, 3], ALU.mult).then_inc(xn4_done, 1)

        def out_half(pool, j, half, before):
            r = j - LAG
            ws = slice(half * HALF, (half + 1) * HALF)
            pool.wait_ge(h_done, 1 + r * W + (half + 1) * HALF)
            pool.wait_ge(ostored, 16 + 32 * r)
            for p in range(2):
                pool.wait_ge(*(before if p == 0 else (ocopy_done, 1 + 4 * r + 2 * half + 1)))
                h = HIST[64 * p:64 * p + 64, ws, :].rearrange("z w (q p) -> z p q w", p=2)[:, p]
                pool.tensor_tensor(OUT[64 * p:64 * p + 64, :, ws], h,
                                   CST[64 * p:64 * p + 64, CHALF:CHALF + 1].unsqueeze(1).broadcast_to([64, Q, HALF]),
                                   ALU.mult).then_inc(ocopy_done, 1)
            pool.wait_ge(ocopy_done, 1 + 4 * r + 2 * half + 2)
            pool.tensor_tensor(OUT[:, :, ws], OUT[:, :, ws], RES4[:, :, ws], ALU.add).then_inc(oadd_done, 1)

        def pool_row(pool, j, involution, lstm):
            if lstm:
                pool.wait_ge(res4n_done, 1 + j)
                pool.wait_ge(oadd_done, 1 + 2 * (j - LAG))
                keep(pool, RES4[:, :, :], RES4_NEXT[:, :, :]).then_inc(res4_done, 1)
            pool.wait_ge(ve_done, 1 + 2 * j + 2)
            pool.wait_ge(rsb_done, 1 + 2 * j)
            rsqrt(pool, RS_Y[:, :, :], RS_T[:, :, :], RS_V[:, :, :], VE[:, :, :], rs_step, 1 + RSN * j)
            pool.wait_ge(rsc_done, 1 + 2 * j + 2)
            pool.wait_ge(logit_done, 1 + j)
            if involution:
                pool.tensor_tensor(XN[:, j + (LEAD + PAD7), :, PAD7:PAD7 + W], XC[:, 0], RSB[:, 0], ALU.mult)
            pool.tensor_tensor(XN2[:, :].rearrange("z (q w) -> z q w", q=Q), XC[:, 1], RSB[:, 1], ALU.mult)
            pool.tensor_tensor(N3[:, j + (N3_TOP - 2), :, 1:1 + W], XC[:, 2], RSB[:, 2], ALU.mult).then_inc(xn_done, 1)
            if lstm:
                pool.wait_ge(res4_done, 1 + j - LAG + 1)
            keep(pool, RES4_NEXT[:, :, :], SL[:, 3]).then_inc(res4n_done, 1)
            if not involution:
                next_inputs(pool, j, lstm)
            if involution:
                a = ACC * j
                for g, (_, _, n) in enumerate(TAPS):
                    if g:
                        pool.wait_ge(prod_done, 1 + NT * j + g + 1)
                        pool.wait_ge(acc_step, 1 + a + g - 1)
                        pool.tensor_tensor(PROD[:, 0, 0:n * TOK], PROD[:, 0, 0:n * TOK], PROD[:, g, 0:n * TOK],
                                           ALU.add).then_inc(acc_step, 1)
                    if g == NT // 2:
                        next_inputs(pool, j, lstm)
                pool.wait_ge(acc_step, 1 + a + NT - 1)
                pool.tensor_tensor(PROD[:, 0, 0:2 * TOK], PROD[:, 0, 0:2 * TOK], PROD[:, 0, 2 * TOK:4 * TOK],
                                   ALU.add).then_inc(acc_step, 1)
                pool.wait_ge(acc_step, 1 + a + NT)
                pool.tensor_tensor(PROD[:, 0, 0:TOK], PROD[:, 0, 0:TOK], PROD[:, 0, TOK:2 * TOK],
                                   ALU.add).then_inc(acc_step, 1)
                pool.wait_ge(acc_step, 1 + a + NT + 1)
                pool.tensor_tensor(PROD[:, 0, 0:TOK], PROD[:, 0, 0:TOK],
                                   X[:, j, :, :].rearrange("z q w -> z (q w)"), ALU.add).then_inc(acc_step, 1)
            if lstm:
                out_half(pool, j, 0, (acc_step, 1 + ACC * j + NT + 2) if involution else (xn4_done, 1 + j + 1))
            if involution:
                pool.tensor_copy(SL[:, 0], X[:, j + LAG, :, :])
            pool.wait_ge(slot2_done, 1 + j + 1)
            if involution:
                pool.wait_ge(acc_step, 1 + ACC * j + NT + 2)
                keep(pool, SL[:, 1], PROD[:, 0, 0:TOK].rearrange("z (q w) -> z q w", q=Q)).then_inc(slot1_done, 1)
            else:
                keep(pool, SL[:, 1], const(CZERO, SL[:, 1])).then_inc(slot1_done, 1)
            if lstm:
                out_half(pool, j, 1, (slot1_done, 1 + j + 1))

        @block.gpsimd
        def _(pool):
            pool.memset(W1C[:, :, :, :], 0.0).then_inc(set_pool, 1)
            pool.memset(W2T[:, :], 0.0).then_inc(set_pool, 1)
            pool.memset(GW[:, :, :], 0.0).then_inc(set_pool, 1)
            for k, v in ((CMHALF, -0.5), (C15, 1.5), (CONE, 1.0), (CZERO, 0.0), (CHALF, 0.5)):
                last = pool.memset(CST[:, k:k + 1], v)
            last.then_inc(set_pool, 1)
            pool.memset(UW[:, :, :, :, :], 0.0).then_inc(set_pool, 1)
            pool.memset(ID[:, :], 0.0).then_inc(set_pool, 1)
            pool.wait_ge(set_pool, 6)
            pool.affine_select(out=ID[:, :], in_=ID[:, :], compare_op=ALU.not_equal, fill=1.0, base=0,
                               pattern=[[-1, 128]], channel_multiplier=1).then_inc(set_pool, 1)
            pool.memset(PM3[:, :, :], 1.0).then_inc(set_pool, 1)
            pool.wait_ge(set_pool, 8)
            pool.affine_select(out=PM3[:, :, :], in_=PM3[:, :, :], compare_op=ALU.is_ge, fill=0.0, base=0,
                               pattern=[[-32, 3], [-CR, 2]], channel_multiplier=1).then_inc(set_pool, 1)
            pool.wait_ge(set_pool, 9)
            pool.affine_select(out=PM3[:, :, :], in_=PM3[:, :, :], compare_op=ALU.is_ge, fill=0.0, base=CR - 1,
                               pattern=[[32, 3], [CR, 2]], channel_multiplier=-1).then_inc(set_pool, 1)
            pool.iota(IOTI[:, :], pattern=[[1, E]], base=0, channel_multiplier=0).then_inc(set_pool, 1)
            pool.memset(SL[:, :, :, :], 0.0).then_inc(set_pool, 1)
            pool.memset(X[:, H:X_ROWS], 0.0).then_inc(set_pool, 1)
            pool.wait_ge(ld_x, 16 * N_X)
            pool.wait_ge(set_pool, 13)
            pool.tensor_copy(SL[:, 0], X[:, LEAD, :, :]).then_inc(lead_xn, 1)
            pool.wait_ge(ld_inv, 16 * len(inv_loads))
            pool.tensor_scalar(BNT[:, 0:1], BNV[:, 3:4], BN_EPS, None, ALU.add).then_inc(set_pool, 1)
            pool.memset(BNT[:, 1:2], -0.5).then_inc(set_pool, 1)
            pool.wait_ge(set_pool, 15)
            pool.tensor_tensor(BNT[:, 2:3], BNT[:, 0:1], BNT[:, 1:2], ALU.pow).then_inc(set_pool, 1)
            pool.wait_ge(lead_ve, 1)
            rsqrt(pool, RS_Y[:, :, :], RS_T[:, :, :], RS_V[:, :, :], VE[:, :, :], lead_rs, 0)
            pool.memset(N3[:, :, :, :], 0.0).then_inc(set_pool, 1)
            pool.wait_ge(lead_rsc, 2)
            pool.wait_ge(set_dve, 1)
            for i in range(LEAD):
                pool.tensor_tensor(XN[:, i + PAD7, :, PAD7:PAD7 + W], XC[:, i], RSB[:, i], ALU.mult).then_inc(lead_xn, 1)
            with pool.Fori(0, 1) as j:
                pool_row(pool, j, True, False)
            pool.wait_ge(ld_rest, 16 * N_X)
            with pool.Fori(1, LAG) as j:
                pool_row(pool, j, True, False)
            with pool.Fori(LAG, H) as j:
                pool_row(pool, j, True, True)
            with pool.Fori(H, H + LAG) as j:
                pool_row(pool, j, False, True)

        def act_fill(act, j, t, involution, lstm, experts):
            if t == MEAN_AT[1] + 1:
                act.wait_ge(xc_done, 1 + j + 1)
                act.activation(SQ[:, :, :, :], XC[:, :, :, :], ACT.Square).then_inc(sq_done, 1)
            if t == VAR_AT[1]:
                act.wait_ge(var_done, 1 + j + 1)
                act.wait_ge(rs_step, 1 + RSN * j)
                vb = H2B[0:TOK, 0:8].rearrange("z (s p) -> z s p", s=4)
                for k, eps in ((0, LN_C_EPS), (1, LN_T_EPS)):
                    act.activation(VE[:, k:4:2], vb[:, k:4:2], ACT.Copy, bias=eps).then_inc(ve_done, 1)
            for k in range(2):
                if t == RSB_AT[k]:
                    act.wait_ge(rsb_done, 1 + 2 * j + k + 1)
                    if k == 0:
                        act.wait_ge(xn4_done, 1 + j)
                    act.activation(RSB[:, 2 * k:2 * k + 2].rearrange("z s q w -> z (s q w)"),
                                   (H2B, YB)[k][:, 0:2 * TOK], ACT.Copy).then_inc(rsc_done, 1)
            if t == CONV1_AT and involution:
                act.wait_ge(conv1_done, 1 + j + 1)
                act.wait_ge(redlo_done, 1 + j)
                act.wait_ge(tap_done, 1 + NT * j)
                for dst, a in ((RED, 0), (REDF, 64)):
                    act.activation(dst[a:96, :], TAPB[a:96, 0:TOK], ACT.Relu, scale=BN[a:96, 0:1], bias=BN[a:96, 1:2])\
                        .then_inc(relu_done, 1)
            if t == DUP_AT + 1:
                act.wait_ge(dup_done, 1 + j + 1)
                act.activation(XS[0:64, :], H1B[0:64, 0:2 * TOK], ACT.Copy).then_inc(xhi_done, 1)
                act.activation(XH[64:128, :], H1B[64:128, 0:2 * TOK], ACT.Copy).then_inc(xhi_done, 1)
            if t == LOGIT_AT + 3:
                act.wait_ge(ngmax_done, 1 + j + 1)
                for p in range(2):
                    act.activation(EX[:, p, :], LG[:, p, :], ACT.Exp, bias=NMX[:, p:p + 1]).then_inc(exp_done, 1)
            if t == dt_at(lstm):
                act.wait_ge(dT_done, 1 + j + 1)
                act.wait_ge(db_done, 1 + NG * j)
                for dst in (DP, DH):
                    act.activation(dst[0:2 * E, :], DB[0:2 * E, 0:TOK], ACT.Copy).then_inc(dp_step, 1)
            k, r = divmod(t - EX0, EXP)
            if r == 0 and 0 <= k < NG and experts:
                act.wait_ge(h1_done, 1 + NG * j + k + 1)
                if not lstm:
                    act.wait_ge(u_done, 1 + NG * j + k)
                act.activation(TH[:, :], h1_bank(k, lstm)[:, 0:EG * 2 * TOK], ACT.Tanh, scale=0.5 / WSCALE)\
                    .then_inc(tanh_done, 1)

        def act_row(act, j, involution, lstm, experts=True):
            for t in range(W):
                if lstm:
                    n = (j - LAG) * W + t
                    c, w = divmod(t, HALF)
                    act.wait_ge(gates_done, 1 + n + 1)
                    act.activation(SCAN[t % 2][:, :, 1:4], gi[c][:, w, :, :], ACT.Tanh, scale=1 / GSCALE).then_inc(gact_done, 1)
                    act.activation(TO[:, t % 2, :], go[c][:, w, :], ACT.Tanh, scale=1 / GSCALE).then_inc(oact_done, 1)
                    act.wait_ge(cell_done, 1 + n + 1)
                    act.activation(TC, STATE[:, t % 2, :, 2], ACT.Tanh, scale=0.5).then_inc(tc_done, 1)
                act_fill(act, j, t, involution, lstm, experts)

        @block.scalar
        def _(act):
            for dst, src in x_loads(0, FIRST):
                act.dma_start(dst, src).then_inc(ld_x, 16)
            act.wait_ge(lead_xc, 1)
            act.activation(SQ[:, :, :, :], XC[:, :, :, :], ACT.Square).then_inc(lead_sq, 1)
            act.wait_ge(lead_var, 1)
            act.activation(VE[:, :, :], H2B[0:TOK, 0:8].rearrange("z (s p) -> z s p", s=4), ACT.Copy, bias=LN_C_EPS)\
                .then_inc(lead_ve, 1)
            act.wait_ge(lead_rsb, 1)
            for k in range(2):
                act.activation(RSB[:, 2 * k:2 * k + 2].rearrange("z s q w -> z (s q w)"), (H2B, YB)[k][:, 0:2 * TOK],
                               ACT.Copy).then_inc(lead_rsc, 1)
            act.wait_ge(ld_exp, 16 * len(exp_loads))
            for k in range(2):
                act.activation(WM[:, k, 0], staged[k], ACT.Copy, scale=WSCALE).then_inc(wm_hi, 1)
            act.wait_ge(set_dve, 3)
            with act.Fori(0, 1) as j:
                act_row(act, j, True, False, experts=False)
            with act.Fori(1, LAG) as j:
                act_row(act, j, True, False)
            with act.Fori(LAG, H) as j:
                act_row(act, j, True, True)
            with act.Fori(H, H + LAG) as j:
                act_row(act, j, False, True)

        def window(row_j, i, j0, n):
            a = XN[:, row_j + i, :, j0:j0 + W]
            return bass.AP(a.tensor, a.offset, [a.ap[0], [1, n], a.ap[1], a.ap[2]])

        GAT = len(GATE_AT)

        def gating(dve, j, k):
            if k:
                dve.wait_ge(gat_step, 1 + GAT * j + k)
            logits = DB[0:TOK, 0:2 * E].rearrange("z (p e) -> z p e", p=2)
            pair = [TOK, 2, 2, E]
            if k == 0:
                dve.wait_ge(logit_done, 1 + j + 1)
                dve.tensor_copy(LG[:, :, :], logits)
                for p in range(2):
                    last = dve.max(MX[:, p, :], logits[:, p, :])
            elif k == 1:
                dve.tensor_scalar(NMX[:, :], MX[:, :, 0], -1.0, None, ALU.mult).then_inc(ngmax_done, 1)
                for p in range(2):
                    last = dve.max_index(IX[:, p, :], MX[:, p, :], LG[:, p, :])
            elif k == 2:
                last = dve.tensor_copy(IXF[:, :, :], IX[:, :, :])
            elif k == 3:
                last = dve.tensor_tensor(DM[:, :, :, :], IOT[:, :].unsqueeze(1).unsqueeze(1).broadcast_to(pair),
                                         IXF[:, :, 0:2].rearrange("z p m -> z m p").unsqueeze(3).broadcast_to(pair),
                                         ALU.is_equal)
            elif k == 4:
                dve.wait_ge(exp_done, 1 + 2 * j + 2)
                last = dve.tensor_tensor(DM[:, :, :, :], DM[:, :, :, :], EX[:, :, :].unsqueeze(1).broadcast_to(pair),
                                         ALU.mult)
            elif k == 5:
                last = dve.tensor_tensor(D1[:, :, :], DM[:, 0], DM[:, 1], ALU.add)
            elif k == 6:
                last = dve.tensor_reduce(DS[:, :], D1[:, :, :], AX.X, ALU.add)
            elif k == 7:
                last = dve.reciprocal(DR[:, :], DS[:, :])
            elif k == 8:
                dve.wait_ge(dT_done, 1 + j)
                last = dve.tensor_tensor(DD[:, :, :], D1[:, :, :], DR[:, :].unsqueeze(2).broadcast_to([TOK, 2, E]), ALU.mult)
            last.then_inc(gat_step, 1)

        def digits_rest(dve, j):
            dve.wait_ge(xhi_done, 1 + 2 * j + 2)
            dve.tensor_tensor(XS[64:128, :], H1B[64:128, 0:2 * TOK], XH[64:128, :], ALU.subtract).then_inc(xslo_done, 1)

        def dve_fill_a(dve, j, t, involution, lstm, experts):
            if t == MEAN_AT[1] + 1:
                dve.wait_ge(mean_done, 1 + j + 1)
                dve.wait_ge(xn4_done, 1 + j)
                dve.tensor_tensor(XC[:, :, :, :].rearrange("z s q w -> z (s q w)"),
                                  SL[:, :, :, :].rearrange("z s q w -> z (s q w)"), H1B[:, 0:4 * TOK], ALU.subtract)\
                    .then_inc(xc_done, 1)
            if involution and t - 1 in tap_at(lstm):
                g = tap_at(lstm).index(t - 1)
                i, j0, n = TAPS[g]
                dve.wait_ge(tap_done, 1 + NT * j + g + 1)
                dve.tensor_tensor(PROD[:, g, 0:n * TOK].rearrange("z (k q w) -> z k q w", k=n, q=Q),
                                  tap_bank(g, lstm)[:, 0:n * TOK].rearrange("z (k q w) -> z k q w", k=n, q=Q),
                                  window(j, i, j0, n), ALU.mult).then_inc(prod_done, 1)
            for k in range(GAT):
                if GATE_AT[k] == f"{t}a":
                    gating(dve, j, k)
                    if k == 2:
                        digits_rest(dve, j)
            if not experts:
                return
            k, r = divmod(t - EX0, EXP)
            if r == 2 and 0 <= k < NG:
                dve.wait_ge(tanh_done, 1 + NG * j + k + 1)
                dve.wait_ge(v_done, 1 + NG * j + k)
                dve.scalar_tensor_tensor(out=UU[:, :], in0=TH[:, :], scalar=1.0, in1=h1_bank(k, lstm)[:, 0:EG * 2 * TOK],
                                         op0=ALU.add, op1=ALU.mult).then_inc(u_done, 1)
            if r == 0 and 0 <= k - 1 < NG:
                dve.wait_ge(h2_done, 1 + NG * j + k)
                dve.wait_ge(u_done, 1 + NG * j + k)
                dve.wait_ge(hd_done, 1 + NG * j + k - 1)
                dve.tensor_tensor(VV[:, :], UU[:, :], H2B[:, 0:EG * 2 * TOK], ALU.mult).then_inc(v_done, 1)
            if r == 1 and 0 <= k - 1 < NG:
                dve.wait_ge(db_done, 1 + NG * j + k)
                dve.wait_ge(v_done, 1 + NG * j + k)
                dve.wait_ge(w3_done, 1 + NG * j + k - 1)
                dve.tensor_tensor(HD[:, :, :, :].rearrange("z e p n -> z (e p n)"), VV[:, :], DB[:, 0:EG * 2 * TOK],
                                  ALU.mult).then_inc(hd_done, 1)

        def dve_fill_b(dve, j, t, involution, lstm):
            if t == CONV1_AT + 1 and involution:
                dve.wait_ge(relu_done, 1 + 2 * j + 2)
                dve.tensor_tensor(RED[64:96, :], REDF[64:96, :], RED[64:96, :], ALU.subtract).then_inc(redlo_done, 1)
            for k in range(GAT):
                if GATE_AT[k] == f"{t}b":
                    gating(dve, j, k)
            if t == dt_at(lstm) + 1:
                dve.wait_ge(dp_step, 1 + 3 * j + 2)
                dve.tensor_tensor(DP[32:64, :], DB[0:32, 0:TOK], DH[:, :], ALU.subtract).then_inc(dp_step, 1)

        def dve_end(dve, j, t, experts):
            if t == OUT3_AT:
                dve.wait_ge(conv_done, 1 + j + 1)
                dve.wait_ge(res4n_done, 1 + j + 1)
                dve.scalar_tensor_tensor(out=SL[:, 3], in0=TAPB[:, 0:TOK].rearrange("z (q w) -> z q w", q=Q),
                                         scalar=CB[:, 0:1], in1=RES3[:, :, :], op0=ALU.add, op1=ALU.add)\
                    .then_inc(slot3_done, 1)
            if t == RES3_AT:
                dve.wait_ge(slot3_done, 1 + j + 1)
                dve.tensor_copy(RES3[:, :, :], SL[:, 2]).then_inc(res3_done, 1)
            if t == OUT2_AT:
                dve.wait_ge(w3_done, 1 + NG * (j + 1))
                dve.wait_ge(res3_done, 1 + j + 1)
                if experts:
                    dve.tensor_tensor(SL[:, 2], SL[:, 1], YB[:, 0:TOK].rearrange("z (q w) -> z q w", q=Q), ALU.add)\
                        .then_inc(slot2_done, 1)
                else:
                    dve.tensor_copy(SL[:, 2], SL[:, 1]).then_inc(slot2_done, 1)

        def dve_row(dve, j, involution, lstm, experts=True):
            for t in range(W):
                n = (j - LAG) * W + t if lstm else None
                dve_fill_a(dve, j, t, involution, lstm, experts)
                if lstm:
                    dve.wait_ge(gact_done, 1 + n + 1)
                    dve.wait_ge(hc_done, 1 + n)
                    flat = SCAN[t % 2][:, :, :].rearrange("z b k -> z (b k)")
                    dve.tensor_tensor_scan(STATE[:, t % 2, :, :].rearrange("z b k -> z (b k)"), flat[:, 0:6 * B:2],
                                           flat[:, 1:6 * B:2], 0.0, op0=ALU.mult, op1=ALU.add).then_inc(cell_done, 1)
                dve_fill_b(dve, j, t, involution, lstm)
                dve_end(dve, j, t, experts)
                if lstm:
                    dve.wait_ge(tc_done, 1 + n + 1)
                    dve.wait_ge(oact_done, 1 + n + 1)
                    for dst, done in ((HHI, hhi_done), (HIST, h_done)):
                        dve.scalar_tensor_tensor(out=dst[:, t, :], in0=TO[:, t % 2, :], scalar=1.0, in1=TC,
                                                 op0=ALU.add, op1=ALU.mult).then_inc(done, 1)
                    dve.wait_ge(h_done, 1 + n + 1)
                    dve.tensor_tensor(HLO[:, t, :], HIST[:, t, :], HHI[:, t, :], ALU.subtract).then_inc(hlo_done, 1)
                    dve.scalar_tensor_tensor(out=SCAN[(t + 1) % 2][:, :, 5], in0=HIST[:, t, :], scalar=0.5,
                                             in1=STATE[:, t % 2, :, 2], op0=ALU.mult, op1=ALU.mult).then_inc(hc_done, 1)
                    if t == EX0:
                        dve.wait_ge(ocopy_done, 1 + 4 * (j - LAG))
                    if t == W - 3:
                        dve.wait_ge(ocopy_done, 1 + 4 * (j - LAG) + 2)

        @block.vector
        def _(dve):
            step = [0]

            def link(ins):
                step[0] += 1
                ins.then_inc(setup_step, 1)
                dve.wait_ge(setup_step, step[0])

            link(dve.memset(MEAN[:, :], 0.0))
            link(dve.memset(MEAN[0:64, 0:64], 1.0 / C))
            link(dve.memset(MEAN[64:128, 64:128], 1.0 / C))
            link(dve.memset(MEAN2[:, :], 0.0))
            for p in range(2):
                last = dve.memset(MEAN2[64 * p:64 * p + 64, p:p + 1], 1.0 / C)
            last.then_inc(mean_set, 1)
            dve.memset(XN[:, 0:PAD7], 0.0)
            dve.memset(XN[:, PAD7:, :, 0:PAD7], 0.0)
            dve.memset(XN[:, PAD7:, :, PAD7 + W:], 0.0).then_inc(set_dve, 1)
            dve.wait_ge(lead_mean, 1)
            dve.tensor_tensor(XC[:, :, :, :], X[:, 0:LEAD], H1B[:, 0:4 * TOK].rearrange("z (s q w) -> z s q w", s=4, q=Q),
                              ALU.subtract).then_inc(lead_xc, 1)
            for tile_, v in ((REP, 0.0), (PM, 1.0), (MHI, 0.0), (MLO, 0.0), (RED, 1.0), (ONE, 1.0)):
                link(dve.memset(tile_[:], v))
            dve.wait_ge(ld_inv, 16 * len(inv_loads))
            dve.wait_ge(set_pool, 16)
            link(dve.tensor_tensor(BNS[:, 0:1], BNV[:, 0:1], BNT[:, 2:3], ALU.mult))
            link(dve.tensor_tensor(BNT[:, 3:4], BNS[:, 0:1], BNV[:, 2:3], ALU.mult))
            link(dve.tensor_tensor(BNS[:, 1:2], BNV[:, 1:2], BNT[:, 3:4], ALU.subtract))
            link(dve.tensor_copy(REP[0:CR, 0:96].rearrange("z (a o) -> z a o", a=6),
                                 ID[0:CR, 0:CR].unsqueeze(1).broadcast_to([CR, 6, CR])))
            dve.memset(REP[32:33, 96:98], 1.0).then_inc(rep_set, 1)
            for p, h in enumerate(halves):
                for rep in (1, 2):
                    link(dve.tensor_copy(W1C[h, rep, p, :], W1C[h, 0, p, :]))
            link(dve.tensor_reduce(PM[0:96, :], PM3[:, :, :].rearrange("z r p -> z p r"), AX.X, ALU.add))
            link(dve.memset(MHI[0:32, :], 1.0))
            link(dve.memset(MHI[64:97, :], 1.0))
            link(dve.memset(MLO[32:64, :], 1.0))
            link(dve.tensor_copy(MLO[96:128, :], ID[96:128, 97:98]))
            dve.wait_ge(set_pe, 1)
            link(dve.tensor_copy(BN[:, :], DB[0:96, 256:258]))
            link(dve.tensor_copy(W2HI[:, :], DB[:, 0:G * K7 * K7]))
            link(dve.tensor_tensor(W2LO[:, :], DB[:, 0:G * K7 * K7], W2HI[:, :], ALU.subtract))
            link(dve.tensor_scalar(W2A[:, :], W2HI[:, :], MHI[:, 0:1], None, ALU.mult))
            link(dve.scalar_tensor_tensor(out=W2A[:, :], in0=W2LO[:, :], scalar=MLO[:, 0:1], in1=W2A[:, :],
                                          op0=ALU.mult, op1=ALU.add))
            for p in range(2):
                link(dve.tensor_scalar(W2M[:, p].rearrange("z g k -> z (g k)"), W2A[:, :], PM[:, p:p + 1], None, ALU.mult))
            for p in range(2):
                for g in range(G):
                    link(dve.tensor_copy(WT[:, :, p, g, :],
                                         W2M[:, p, g, :].unsqueeze(2).broadcast_to([128, K7 * K7, GC])))
            for tile_, v in ((DP, 0.0), (RES3, 0.0), (HIST, 0.0), (HHI, 0.0), (HLO, 0.0), (SCAN[0], 0.0), (SCAN[1], 0.0),
                             (WC, 0.0), (IDUP, 0.0)):
                link(dve.memset(tile_[:], v))
            for k in range(2):
                link(dve.memset(SCAN[k][:, :, 4:5], 1.0))
            link(dve.tensor_copy(IOT[:, :], IOTI[:, :]))
            for p, h in enumerate(halves):
                for m in range(2):
                    link(dve.tensor_copy(IDUP[h, p, 64 * m:64 * m + 64], ID[h, h]))
            dve.wait_ge(ld_w, 16 * len(w_loads))
            for k, a in enumerate((GSCALE, 0.5 * GSCALE, 0.5 * GSCALE)):
                link(dve.tensor_scalar(UW[:, :, k], UW[:, :, k], a, None, ALU.mult))
                link(dve.tensor_scalar(BW[:, k], BW[:, k], a, None, ALU.mult))
            dve.wait_ge(wm_hi, 2)
            for k in range(2):
                dve.scalar_tensor_tensor(out=WM[:, k, 1], in0=staged[k], scalar=WSCALE, in1=WM[:, k, 0],
                                         op0=ALU.mult, op1=ALU.subtract).then_inc(wm_lo, 1)
            dve.wait_ge(set_pe, 2)
            for h in halves:
                link(dve.tensor_scalar(WC[h, 0:8, h], H1B[0:64, 0:8 * C].rearrange("z (k c) -> z k c", k=8),
                                       1.0 / (2 * TERMS), None, ALU.mult))
                dve.tensor_scalar(WC[h, 8, h], H2B[0:64, 0:C], 1.0 / (2 * TERMS), None, ALU.mult).then_inc(set_dve, 1)
            dve.wait_ge(wm_lo, 2)
            with dve.Fori(0, 1) as j:
                dve_row(dve, j, True, False, experts=False)
            for a in (0, 32):
                link(dve.tensor_copy(SEL[a:a + 2 * E, :, :, :].rearrange("z p e n -> z (p e) n"),
                                     ID[a:a + 2 * E, a:a + 2 * E].unsqueeze(2).broadcast_to([2 * E, 2 * E, HID])))
            link(dve.tensor_scalar(W3[:, :, :], W3[:, :, :], 0.5 / (WSCALE * WSCALE), None, ALU.mult))
            for k, a in enumerate((0.5 * GSCALE, 0.25 * GSCALE, 0.25 * GSCALE)):
                link(dve.tensor_scalar(VF[:, k, :], VF[:, k, :], a, None, ALU.mult))
            link(dve.tensor_copy(VH[:, :, :], VF[:, :, :]))
            for m in range(2):
                link(dve.tensor_copy(VW[0:64, :, m, :], VF[0:64, :, :]))
                last = dve.tensor_tensor(VW[64:128, :, m, :], VF[64:128, :, :], VH[64:128, :, :], ALU.subtract)
            last.then_inc(set_dve, 1)
            dve.wait_ge(set_dve, 4)
            with dve.Fori(1, LAG) as j:
                dve_row(dve, j, True, False)
            dve.wait_ge(u_done, 1 + NG * LAG)
            dve.memset(STATE, 0.0).then_inc(set_dve, 1)
            dve.wait_ge(set_dve, 5)
            with dve.Fori(LAG, H) as j:
                dve_row(dve, j, True, True)
            with dve.Fori(H, H + LAG) as j:
                dve_row(dve, j, False, True)

        def prefill(pe, c, k):
            bw = BW[:, :, :, :].rearrange("z k m c -> z k (m c)")
            uw = UW[:, :, :, :, :].rearrange("z p k m c -> z p k (m c)")
            out_g = go[c].rearrange("z t b -> z (t b)")
            gates = gi[c].rearrange("z t b k -> z (t b) k")
            n = HALF * B
            if k < 4:
                o, g = ((out_g, 2), (gates[:, :, 1], 1), (gates[:, :, 0], 0), (gates[:, :, 2], 0))[k]
                return pe.matmul(o, bw[0:1, g], ONE[0:1, 0:n], start=(k == 0), stop=False, skip_group_check=True)
            p, g = divmod(k - 4, 3)
            r = XN4[:, :, c * HALF:(c + 1) * HALF]
            xg = gi[c].rearrange("z t (q p) k -> z p q t k", p=2)[:, p]
            if g == 0:
                o, r = xg[:, :, :, 0:3:2], r.unsqueeze(3).broadcast_to([128, Q, HALF, 2])
            else:
                o = xg[:, :, :, 1] if g == 1 else go[c].rearrange("z t (q p) -> z p q t", p=2)[:, p]
            return pe.matmul(o, uw[:, p, g], r, start=False, stop=False, skip_group_check=True)

        RS_BANKS = (H2B, YB)

        def variances(pe, a, b):
            for k in range(a, b):
                last = pe.matmul(H2B[0:TOK, 2 * k:2 * k + 2], SQ[:, k].rearrange("z q w -> z (q w)"), MEAN2[:, :],
                                 start=True, stop=True, skip_group_check=True)
            return last

        def spread_rs(pe, a, b):
            for k in range(a, b):
                last = pe.matmul(RS_BANKS[k // 2][:, (k % 2) * TOK:(k % 2 + 1) * TOK], RSE[:, k].rearrange("z p c -> z (p c)"),
                                 ID[0:TOK, 0:TOK], start=True, stop=True, skip_group_check=True)
            return last

        def pe_fill(pe, j, t, involution, lstm, experts):
            if t == CONV1_AT and involution:
                pe.wait_ge(slot3_done, 1 + j)
                pe.matmul(TAPB[0:96, 0:TOK], W1C[:, :, :, :].rearrange("z r p o -> z (r p o)"),
                          XN[:, j + PAD7, :, PAD7:PAD7 + W], start=True, stop=True).then_inc(conv1_done, 1)
            for k in range(2):
                if t == MEAN_AT[k]:
                    if k == 0:
                        pe.wait_ge(slot1_done, 1 + j)
                        pe.wait_ge(slot2_done, 1 + j)
                        pe.wait_ge(slot3_done, 1 + j)
                        pe.wait_ge(u_done, 1 + NG * j)
                    n = 2 * k * TOK
                    last = pe.matmul(H1B[:, n:n + 2 * TOK], MEAN[:, :],
                                     SL[:, 2 * k:2 * k + 2].rearrange("z s q w -> z (s q w)"),
                                     start=True, stop=True, skip_group_check=True)
                    if k == 1:
                        last.then_inc(mean_done, 1)
                if t == VAR_AT[k]:
                    if k == 0:
                        pe.wait_ge(sq_done, 1 + j + 1)
                        pe.wait_ge(v_done, 1 + NG * j)
                    last = variances(pe, 2 * k, 2 * k + 2)
                    if k == 1:
                        last.then_inc(var_done, 1)
                if t == RSB_AT[k]:
                    pe.wait_ge(rs_step, 1 + RSN * (j + 1) - 1 + k)
                    spread_rs(pe, 2 * k, 2 * k + 2).then_inc(rsb_done, 1)
            if t == LOGIT_AT:
                pe.wait_ge(xn_done, 1 + j + 1)
                pe.wait_ge(hd_done, 1 + NG * j)
                pe.matmul(DB[0:TOK, 0:2 * E], ONE[0:1, 0:TOK], GB[0:1, :, :].rearrange("z p e -> z (p e)"),
                          start=True, stop=False, skip_group_check=True)
                pe.matmul(DB[0:TOK, 0:2 * E], XN2[:, :], GW[:, :, :].rearrange("z p e -> z (p e)"), start=False, stop=True,
                          skip_group_check=True).then_inc(logit_done, 1)
            if lstm:
                for k in PRE1_AT.get(t, ()):
                    if k == 0:
                        pe.wait_ge(oact_done, 1 + (j - LAG) * W)
                    last = prefill(pe, 1, k)
                    if k == PRODUCTS - 1:
                        last.then_inc(pre1_done, 1)
            if t == dt_at(lstm):
                pe.wait_ge(gat_step, 1 + GAT * (j + 1))
                pe.matmul(DB[0:2 * E, 0:TOK], DD[:, :, :].rearrange("z p e -> z (p e)"), ID[0:TOK, 0:TOK], start=True,
                          stop=True, skip_group_check=True).then_inc(dT_done, 1)
            if involution and t in tap_at(lstm):
                g = tap_at(lstm).index(t)
                if g == 0:
                    pe.wait_ge(redlo_done, 1 + j + 1)
                    pe.wait_ge(relu_done, 1 + 2 * j + 2)
                i, j0, n = TAPS[g]
                pe.wait_ge(prod_done, 1 + NT * j + g - (1 if g and not lstm else 0))
                for m in range(n):
                    last = pe.matmul(tap_bank(g, lstm)[:, m * TOK:(m + 1) * TOK],
                                     WT[:, i * K7 + j0 + m].rearrange("z p g c -> z (p g c)"), RED[:, :],
                                     start=(m == 0), stop=True, skip_group_check=True)
                last.then_inc(tap_done, 1)
            if t == DUP_AT:
                pe.wait_ge(xc_done, 1 + j + 1)
                for p in range(2):
                    last = pe.matmul(H1B[:, p * TOK:(p + 1) * TOK], IDUP[:, p, :], XN2[:, :], start=True, stop=True,
                                     skip_group_check=True)
                last.then_inc(dup_done, 1)
            k, r = divmod(t - EX0, EXP) if experts else (-EXP, 0)
            if r == 0 and 0 <= k < NG:
                if k == 0:
                    pe.wait_ge(xslo_done, 1 + j + 1)
                    pe.wait_ge(xhi_done, 1 + 2 * j + 2)
                pe.wait_ge(u_done, 1 + NG * j + k - (1 if k and not lstm else 0))
                expert_in(pe, h1_bank(k, lstm), 0, k).then_inc(h1_done, 1)
            if r == 1 and 0 <= k < NG:
                pe.wait_ge(v_done, 1 + NG * j + k)
                expert_in(pe, H2B, 1, k).then_inc(h2_done, 1)
            if r == 2 and 0 <= k < NG:
                pe.wait_ge(hd_done, 1 + NG * j + k)
                if k == 0:
                    pe.wait_ge(dp_step, 1 + 3 * j + 3)
                spread_weights(pe, k, 0)
                if not lstm:
                    spread_weights(pe, k, 1).then_inc(db_done, 1)
            if r == 0 and 0 <= k - 1 < NG and lstm:
                spread_weights(pe, k - 1, 1).then_inc(db_done, 1)
            if r == 2 and 0 <= k - 1 < NG:
                pe.wait_ge(hd_done, 1 + NG * j + k)
                if k == 1:
                    pe.wait_ge(slot2_done, 1 + j)
                for m in range(EG):
                    for p in range(2):
                        last = pe.matmul(YB[64 * p:64 * p + 64, 0:TOK], W3[:, EG * (k - 1) + m, :], HD[:, m, p, :],
                                         start=(k == 1 and m == 0), stop=(k == NG and m == EG - 1), skip_group_check=True)
                last.then_inc(w3_done, 1)
            if t in CONV_AT:
                k = CONV_AT.index(t)
                di, dj = divmod(k, 3)
                if k == 0:
                    pe.wait_ge(xn_done, 1 + j + 1)
                    if involution:
                        pe.wait_ge(prod_done, 1 + NT * j + NT)
                    else:
                        pe.wait_ge(slot3_done, 1 + j)
                last = pe.matmul(TAPB[:, 0:TOK], WC[:, k, :], N3[:, j + (N3_TOP - 4 + di), :, dj:dj + W],
                                 start=(k == 0), stop=(k == 8), skip_group_check=True)
                if k == 8:
                    last.then_inc(conv_done, 1)
            for k in PRE0_AT.get(t, ()):
                if k == 0:
                    pe.wait_ge(xn4_done, 1 + j + 1)
                    if lstm:
                        pe.wait_ge(oact_done, 1 + (j - LAG) * W + HALF)
                last = prefill(pe, 0, k)
                if k == PRODUCTS - 1:
                    last.then_inc(pre0_done, 1)

        def spread_weights(pe, k, m):
            for p in range(2):
                last = pe.matmul(DB[:, (2 * m + p) * TOK:(2 * m + p + 1) * TOK], SEL[:, p, EG * k + m, :], DP[:, :],
                                 start=(m == 0 and p == 0), stop=True, skip_group_check=True)
            return last

        def expert_in(pe, bank, which, k):
            for m in range(EG):
                for part in range(2):
                    last = pe.matmul(bank[:, m * 2 * TOK:(m + 1) * 2 * TOK], WM[:, which, part, EG * k + m, :], XS[:, :],
                                     start=(m == 0 and part == 0), stop=(part == 1), skip_group_check=True)
            return last

        def pe_row(pe, j, involution, lstm, experts=True):
            for t in range(W):
                if lstm:
                    n = (j - LAG) * W + t
                    c, w = divmod(t, HALF)
                    for digits, done in ((HHI, hhi_done), (HLO, hlo_done)):
                        h = digits[:, (t - 1) % W, :]
                        pe.wait_ge(done, 1 + n)
                        pe.matmul(go[c][:, w, :], VW[:, 2].rearrange("z m c -> z (m c)"), h, start=False, stop=True,
                                  skip_group_check=True)
                        pe.matmul(gi[c][:, w, :, 0:3:2], VW[:, 0].rearrange("z m c -> z (m c)"),
                                  h.unsqueeze(2).broadcast_to([128, B, 2]), start=False, stop=True, skip_group_check=True)
                        last = pe.matmul(gi[c][:, w, :, 1], VW[:, 1].rearrange("z m c -> z (m c)"), h, start=False,
                                         stop=True, skip_group_check=True)
                    last.then_inc(gates_done, 1)
                pe_fill(pe, j, t, involution, lstm, experts)

        @block.tensor
        def _(pe):
            pe.wait_ge(mean_set, 1)
            pe.wait_ge(ld_x, 16 * N_X)
            pe.matmul(H1B[:, 0:4 * TOK], MEAN[:, :], X[:, 0:LEAD].rearrange("z s q w -> z (s q w)"), start=True, stop=True)\
                .then_inc(lead_mean, 1)
            pe.wait_ge(lead_sq, 1)
            variances(pe, 0, LEAD).then_inc(lead_var, 1)
            pe.wait_ge(set_pool, 7)
            pe.wait_ge(lead_rs, RSN)
            spread_rs(pe, 0, LEAD).then_inc(lead_rsb, 1)
            pe.wait_ge(rep_set, 1)
            pe.matmul(DB[:, 0:G * K7 * K7], REP[:, :], W2T[:, :], start=True, stop=True, skip_group_check=True)
            pe.matmul(DB[0:96, 256:258], REP[0:CR, 0:96], BNS[:, :], start=True, stop=True, skip_group_check=True)\
                .then_inc(set_pe, 1)
            pe.wait_ge(ld_w, 16 * len(w_loads))
            pe.wait_ge(lead_xc, 1)
            pe.wait_ge(lead_rsc, 2)
            for k in range(9):
                bank, a = (H1B, C * k) if k < 8 else (H2B, 0)
                o = bank[0:64, a:a + C]
                last = pe.matmul(o, S1[:, :, k], U1[:, :], start=True, stop=False, skip_group_check=True)
                for m in range(NK):
                    last = pe.matmul(o, U2[:, m, :, k], S2[:, m, :], start=False, stop=(m == NK - 1), skip_group_check=True)
            last.then_inc(set_pe, 1)
            pe.wait_ge(set_dve, 3)
            pe.wait_ge(lead_xn, 1 + LEAD)
            with pe.Fori(0, 1) as j:
                pe_row(pe, j, True, False, experts=False)
            pe.wait_ge(set_dve, 4)
            with pe.Fori(1, LAG) as j:
                pe_row(pe, j, True, False)
            with pe.Fori(LAG, H) as j:
                pe_row(pe, j, True, True)
            with pe.Fori(H, H + LAG) as j:
                pe_row(pe, j, False, True)


_INS = ["x", "L0_conv_conv1_w", "L0_conv_bn_gamma", "L0_conv_bn_beta", "L0_conv_bn_mean", "L0_conv_bn_var",
        "L0_conv_conv2_w", "L0_conv_conv2_b", "L0_ffn_gate_w", "L0_ffn_gate_b", "L0_ffn_w1", "L0_ffn_w2", "L0_ffn_w3",
        "L1_conv_S1s", "L1_conv_S2s", "L1_conv_U1s", "L1_conv_U2s", "L1_conv_bias",
        "L1_ffn_U_i", "L1_ffn_V_i", "L1_ffn_b_i", "L1_ffn_U_c", "L1_ffn_V_c", "L1_ffn_b_c",
        "L1_ffn_U_o", "L1_ffn_V_o", "L1_ffn_b_o"]


def kernel(**inputs):
    import numpy as _np
    import concourse.bacc as _bacc
    from concourse import mybir as _mybir
    from concourse.bass_utils import run_bass_kernel_spmd as _run

    nc = _bacc.Bacc("TRN2", target_bir_lowering=False, num_devices=1)
    arrays, args = {}, []
    for name in _INS:
        a = _np.ascontiguousarray(inputs[name])
        arrays[f"in_{name}_dram"] = a
        args.append(nc.dram_tensor(f"in_{name}_dram", a.shape, _mybir.dt.from_np(a.dtype), kind="ExternalInput").ap())
    args.append(nc.dram_tensor("out_0_dram", (B, C, H, W), F32, kind="ExternalOutput").ap())
    build_program(nc, *args)
    r = _run(nc, [arrays], core_ids=[0])
    return r.results[0]["out_0_dram"]
```
